# Optimizing a Trainium2 kernel written in Bass

```python
import numpy as np
import jax
import jax.numpy as jnp

def _softmax(x, axis=-1):
    return jax.nn.softmax(x, axis=axis)

def _gelu(x):
    return jax.nn.gelu(x, approximate=True)

def _silu(x):
    return jax.nn.silu(x)

def _sigmoid(x):
    return jax.nn.sigmoid(x)

def _layernorm(x, axis=-1, eps=1e-05):
    m = jnp.mean(x, axis=axis, keepdims=True)
    v = jnp.var(x, axis=axis, keepdims=True)
    return (x - m) / jnp.sqrt(v + eps)

def _scatter_add(tgt, idx, src, axis=0):
    return tgt.at[idx].add(src)

def _segment_sum(src, seg, n):
    return jax.ops.segment_sum(src, seg, n)
kernel_name = 'mk_adj_resnorm_d4_adj_r2_db8798'

def setup_inputs(seed: int=0):
    np.random.seed(seed)
    _w = jnp.asarray

    def _rec_inputs():
        import jax
        import jax.numpy as jnp
        _gk = jax.random.key(seed)
        x = -0.0002928 + 1 * jax.random.normal(jax.random.fold_in(_gk, 1), (64, 128, 256), jnp.float32)
        _w = (1.0 + jnp.arange(128, dtype=jnp.float32)) ** (-0.5)
        _w = _w / _w.mean()
        _pij = jnp.clip(0.125 * _w[:, None] * _w[None, :], 0.0, 1.0)
        _a = jax.random.uniform(jax.random.fold_in(_gk, 2), (64, 128, 128)) < _pij
        _a = jnp.logical_or(_a, jnp.swapaxes(_a, -1, -2))
        _a = jnp.logical_or(_a, jnp.eye(128, dtype=bool))
        _af = _a.astype(jnp.float32)
        _af = _af * jax.random.uniform(jax.random.fold_in(_gk, 3), (64, 128, 128), jnp.float32, 0.05, 1)
        adj = _af
        return (x, adj)
    x, adj = _rec_inputs()

    def _L0_gnn_setup():
        import jax, jax.numpy as jnp
        import numpy as np
        B, N, DIN, DOUT, K = (4, 1024, 256, 256, 3)
        key = jax.random.key(seed)
        ks = jax.random.split(key, 8)
        X = jax.random.normal(ks[0], (B, N, DIN), dtype=jnp.float32)
        A = jax.random.uniform(ks[1], (B, N, N), dtype=jnp.float32)
        Wv = jax.random.normal(ks[2], (DIN, DOUT), dtype=jnp.float32) * 0.02
        bv = jax.random.normal(ks[3], (DOUT,), dtype=jnp.float32) * 0.02
        aw = jax.random.normal(ks[4], (2 * DOUT, 1), dtype=jnp.float32) * 0.05
        ab = jax.random.normal(ks[5], (1,), dtype=jnp.float32) * 0.05
        Wk = jax.random.normal(ks[6], (K, DIN, DOUT), dtype=jnp.float32) * 0.02
        bk = jax.random.normal(ks[7], (K, DOUT), dtype=jnp.float32) * 0.02
        return {'X': X, 'A': A, 'Wv': Wv, 'bv': bv, 'aw': aw, 'ab': ab, 'Wk': Wk, 'bk': bk}
    _L0_gnn_all = _L0_gnn_setup()
    _L0_gnn_in = {k: v for k, v in _L0_gnn_all.items() if k in ('Wv', 'bv', 'aw', 'ab', 'Wk', 'bk')}
    del _L0_gnn_all

    def _L1_gnn_setup():
        import jax, jax.numpy as jnp
        import numpy as np
        B, N, DIN, DOUT, H = (32, 512, 256, 256, 8)
        DH = DOUT // H
        key = jax.random.key(seed)
        k1, k2, k3, k4, k5 = jax.random.split(key, 5)
        X = jax.random.normal(k1, (B, N, DIN), dtype=jnp.float32)
        A = (jax.random.uniform(k2, (B, N, N)) < 0.05).astype(jnp.float32)
        A = jnp.maximum(A, jnp.eye(N, dtype=jnp.float32)[None])
        std_w = np.sqrt(2.0 / (DIN + DH))
        std_c = np.sqrt(2.0 / (DH + DH))
        Wp = jax.random.normal(k3, (H, DIN, DH), dtype=jnp.float32) * std_w
        bp = jnp.zeros((H, DH), dtype=jnp.float32)
        C = jax.random.normal(k4, (H, DH, DH), dtype=jnp.float32) * std_c
        return {'X': X, 'A': A, 'Wp': Wp, 'bp': bp, 'C': C}
    _L1_gnn_all = _L1_gnn_setup()
    _L1_gnn_in = {k: v for k, v in _L1_gnn_all.items() if k in ('Wp', 'bp', 'C')}
    del _L1_gnn_all

    def _L2_gnn_setup():
        import jax, jax.numpy as jnp
        import numpy as np
        IN_DIM = 256
        ATT_DIM = 64
        B, N = (4, 2048)
        key = jax.random.key(seed)
        k1, k2, k3, k4 = jax.random.split(key, 4)
        x = jax.random.normal(k1, (B, N, IN_DIM), dtype=jnp.float32)
        adj_matrix = (jax.random.uniform(k2, (B, N, N)) < 0.05).astype(jnp.float32)
        W_qk = jax.random.normal(k3, (2 * ATT_DIM, IN_DIM), dtype=jnp.float32) / np.sqrt(IN_DIM)
        W_v = jax.random.normal(k4, (IN_DIM, IN_DIM), dtype=jnp.float32) / np.sqrt(IN_DIM)
        return {'x': x, 'adj_matrix': adj_matrix, 'W_qk': W_qk, 'W_v': W_v}
    _L2_gnn_all = _L2_gnn_setup()
    _L2_gnn_in = {k: v for k, v in _L2_gnn_all.items() if k in ('W_qk', 'W_v')}
    del _L2_gnn_all

    def _L3_gnn_setup():
        import jax, jax.numpy as jnp
        import numpy as np
        B, N, F_IN, F_HID, F_OUT = (32, 512, 256, 256, 256)

        def _gcn_layer(x, adj, W, b):
            support = jnp.einsum('bnf,fh->bnh', x, W)
            return jnp.einsum('bnm,bmh->bnh', adj, support) + b
        key = jax.random.key(seed)
        ks = jax.random.split(key, 8)

        def xavier(k, fan_in, fan_out):
            bound = float(np.sqrt(6.0 / (fan_in + fan_out)))
            return jax.random.uniform(k, (fan_in, fan_out), jnp.float32, -bound, bound)
        return {'batch_graph': jax.random.normal(ks[0], (B, N, F_IN), jnp.float32), 'adj': jax.random.uniform(ks[1], (B, N, N), jnp.float32), 'W1': xavier(ks[2], F_IN, F_HID), 'b1': jnp.zeros((F_HID,), jnp.float32), 'W2': xavier(ks[3], F_HID, F_HID), 'b2': jnp.zeros((F_HID,), jnp.float32), 'W3': xavier(ks[4], F_HID, F_OUT), 'b3': jnp.zeros((F_OUT,), jnp.float32)}
    _L3_gnn_all = _L3_gnn_setup()
    _L3_gnn_in = {k: v for k, v in _L3_gnn_all.items() if k in ('W1', 'b1', 'W2', 'b2', 'W3', 'b3')}
    del _L3_gnn_all
    return {'x': x, 'adj': adj, 'L0_gnn_Wv': _L0_gnn_in['Wv'], 'L0_gnn_bv': _L0_gnn_in['bv'], 'L0_gnn_aw': _L0_gnn_in['aw'], 'L0_gnn_ab': _L0_gnn_in['ab'], 'L0_gnn_Wk': _L0_gnn_in['Wk'], 'L0_gnn_bk': _L0_gnn_in['bk'], 'L1_gnn_Wp': _L1_gnn_in['Wp'], 'L1_gnn_bp': _L1_gnn_in['bp'], 'L1_gnn_C': _L1_gnn_in['C'], 'L2_gnn_W_qk': _L2_gnn_in['W_qk'], 'L2_gnn_W_v': _L2_gnn_in['W_v'], 'L3_gnn_W1': _L3_gnn_in['W1'], 'L3_gnn_b1': _L3_gnn_in['b1'], 'L3_gnn_W2': _L3_gnn_in['W2'], 'L3_gnn_b2': _L3_gnn_in['b2'], 'L3_gnn_W3': _L3_gnn_in['W3'], 'L3_gnn_b3': _L3_gnn_in['b3']}

def reference(x, adj, L0_gnn_Wv, L0_gnn_bv, L0_gnn_aw, L0_gnn_ab, L0_gnn_Wk, L0_gnn_bk, L1_gnn_Wp, L1_gnn_bp, L1_gnn_C, L2_gnn_W_qk, L2_gnn_W_v, L3_gnn_W1, L3_gnn_b1, L3_gnn_W2, L3_gnn_b2, L3_gnn_W3, L3_gnn_b3):
    import jax
    import jax.numpy as jnp

    def _L0_gnn_ref(X, A, Wv, bv, aw, ab, Wk, bk):
        import jax, jax.numpy as jnp
        import numpy as np
        B, N, DIN, DOUT, K = (4, 1024, 256, 256, 3)
        d = Wv.shape[1]
        Xw = X @ Wv + bv
        sj = Xw @ aw[:d, 0]
        si = Xw @ aw[d:, 0]
        e = jax.nn.leaky_relu(sj[:, None, :] + si[:, :, None] + ab[0], negative_slope=0.2)
        alpha_matrix = A * jnp.exp(e)
        transition = alpha_matrix / (jnp.sum(alpha_matrix, axis=-1, keepdims=True) + 1e-12)
        H = jnp.zeros(X.shape[:-1] + (d,), dtype=X.dtype)
        Xk = X
        for k in range(Wk.shape[0]):
            H = H + Xk @ Wk[k] + bk[k]
            Xk = jnp.einsum('bij,bjd->bid', transition, Xk)
        return jax.nn.relu(H)

    def _L1_gnn_ref(X, A, Wp, bp, C):
        import jax, jax.numpy as jnp
        import numpy as np
        B, N, DIN, DOUT, H = (32, 512, 256, 256, 8)
        DH = DOUT // H
        Xp = jnp.einsum('bnd,hdk->bhnk', X, Wp) + bp[None, :, None, :]
        Xc = jnp.einsum('bhnk,hjk->bhnj', Xp, C)
        attn = jnp.tanh(A[:, None] * jnp.einsum('bhnj,bhmj->bhnm', Xc, Xp))
        Xh = jnp.einsum('bhnm,bhmk->bhnk', attn, Xp)
        out = jnp.moveaxis(Xh, 1, 2).reshape(X.shape[0], X.shape[1], -1)
        return jax.nn.relu(out)

    def _L2_gnn_ref(x, adj_matrix, W_qk, W_v):
        import jax, jax.numpy as jnp
        import numpy as np
        IN_DIM = 256
        ATT_DIM = 64
        B, N = (4, 2048)
        qk = jnp.einsum('bnd,ed->bne', x, W_qk)
        q, k = jnp.split(qk, 2, axis=-1)
        v = jnp.einsum('bnd,ed->bne', x, W_v)
        inv_scale = 1.0 / ATT_DIM ** 0.5
        scores = jnp.einsum('bnd,bmd->bnm', q, k) * inv_scale
        w = jnp.sum(scores * adj_matrix, axis=-1, keepdims=True)
        w = jax.nn.softmax(w, axis=1)
        return w * v

    def _L3_gnn_ref(batch_graph, adj, W1, b1, W2, b2, W3, b3):
        import jax, jax.numpy as jnp
        import numpy as np
        B, N, F_IN, F_HID, F_OUT = (32, 512, 256, 256, 256)

        def _gcn_layer(x, adj, W, b):
            support = jnp.einsum('bnf,fh->bnh', x, W)
            return jnp.einsum('bnm,bmh->bnh', adj, support) + b
        x = jax.nn.relu(_gcn_layer(batch_graph, adj, W1, b1))
        x = jax.nn.relu(_gcn_layer(x, adj, W2, b2))
        out = _gcn_layer(x, adj, W3, b3)
        return out
    x = _layernorm(x + _L0_gnn_ref(x, adj, L0_gnn_Wv, L0_gnn_bv, L0_gnn_aw, L0_gnn_ab, L0_gnn_Wk, L0_gnn_bk), axis=-1)
    x = _layernorm(x + _L1_gnn_ref(x, adj, L1_gnn_Wp, L1_gnn_bp, L1_gnn_C), axis=-1)
    x = _layernorm(x + _L2_gnn_ref(x, adj, L2_gnn_W_qk, L2_gnn_W_v), axis=-1)
    x = _layernorm(x + _L3_gnn_ref(x, adj, L3_gnn_W1, L3_gnn_b1, L3_gnn_W2, L3_gnn_b2, L3_gnn_W3, L3_gnn_b3), axis=-1)
    return x

_drawn_inputs = setup_inputs


def setup_inputs(seed=0):
    import zlib

    import numpy as np

    out = dict(_drawn_inputs(seed))
    spreads = {'L1_gnn_bp': (0.0, 0.1),
     'L3_gnn_b1': (0.0, 0.284),
     'L3_gnn_b2': (0.0, 2.0),
     'L3_gnn_b3': (0.0, 2.0)}
    factors = {'L0_gnn_Wv': 3.007, 'L0_gnn_bv': 8.0, 'L0_gnn_aw': 3.047}
    for name, (base, spread) in spreads.items():
        noise = np.random.default_rng([zlib.crc32(name.encode()), seed]).standard_normal(out[name].shape)
        drawn = base * np.exp(spread * noise) if base else spread * noise
        out[name] = jnp.asarray(drawn.astype(out[name].dtype))
    for name, factor in factors.items():
        out[name] = (out[name] * factor).astype(out[name].dtype)
    return out
```

```python
from contextlib import ExitStack

import concourse.bass as bass
from concourse import mybir

F32 = mybir.dt.float32
F32R = mybir.dt.float32r
ALU = mybir.AluOpType
ACT = mybir.ActivationFunctionType
AX_X = mybir.AxisListType.X

P = 128
B = 64
D = 256
C = D // P
G = 4
GROUPS = B // G
PAIRS = G // 2
H = 8
DH = D // H
QH = P // DH
E = 64
QK = 2 * E
EPS = 1e-5
TINY = 1e-12
SLOPE = 0.2

W_Y2, Y2W = 0, D + 2
W_Z = W_Y2 + C * Y2W
W_H = W_Z + C * D
W_P = W_H + C * D
W_QKV, QKVW = W_P + C * D, D + QK
W_S1 = W_QKV + C * QKVW
W_END = W_S1 + C * D


class Turn:

    def __init__(self, engine, group):
        self.engine, self.group, self.known = engine, group, {}

    def wait(self, semaphore, each, k=None):
        k = each if k is None else k
        if isinstance(self.group, int):
            value = self.group * each + k
            if value > 0:
                self.engine.wait_ge(semaphore, value)
            return
        if (each, k) not in self.known:
            self.known[each, k] = self.engine.snap(self.group * each + k)
        self.engine.wait_ge(semaphore, self.known[each, k])


def build(nc, x, xT, aT, wraw, wvT, awc, bvc, ab, bk, bpc, cT, b1c, b2c, w23, b3, out):
    with ExitStack() as ctx:
        def sb(name, shape, dt=F32):
            return ctx.enter_context(nc.sbuf_tensor(name, shape, dt))

        def sem(name):
            return ctx.enter_context(nc.semaphore(name))

        w_raw = sb("w_raw", [P, W_END])
        w_hi = sb("w_hi", [P, W_END], F32R)
        w_lo = sb("w_lo", [P, W_END], F32R)
        wv_t = sb("wv_t", [P, C, D])
        aw_c = sb("aw_c", [P, 2, C])
        bv_c = sb("bv_c", [P, C])
        ab_c = sb("ab_c", [P, 1])
        z_bias = sb("z_bias", [P, 2])
        z_const = sb("z_const", [P, 1])
        bk_row = sb("bk_row", [1, 3, D])
        rows_raw = sb("rows_raw", [1, 2, D])
        rows = sb("rows", [2, 2, D], F32R)
        row_lo = sb("row_lo", [1, 2, D], F32R)
        bp_c = sb("bp_c", [P, C])
        b1_c = sb("b1_c", [P, C])
        b2_c = sb("b2_c", [P, C])
        c_t = sb("c_t", [P, C, P])
        w_23 = sb("w_23", [P, 2, C, D])
        ident = sb("ident", [P, P])
        ones = sb("ones", [P, P])
        ones_r = sb("ones_r", [2, P], F32R)
        neg_half = sb("neg_half", [P, G])
        anchor = sb("anchor", [1, 4])
        act_seed = sb("act_seed", [P, 1])
        xa = sb("xa", [P, G, D])
        xa_t = sb("xa_t", [P, C, G, P])
        xa_hi = sb("xa_hi", [P, C, G, P], F32R)
        xa_lo = sb("xa_lo", [P, C, G, P], F32R)
        adj_a = sb("adj_a", [P, G, P])
        y2 = sb("y2", [P, G, Y2W])
        zsum = sb("zsum", [P, G, P])
        zrelu = sb("zrelu", [P, G, P])
        zexp = sb("zexp", [P, G, P])
        alpha = sb("alpha", [P, G, P])
        rrow = sb("rrow", [P, G, P])
        rden = sb("rden", [P, G, P])
        trans = sb("trans", [P, G, P])
        zed = sb("zed", [P, G, D])
        ya = sb("ya", [P, G, D])
        x1 = sb("x1", [P, G, D])
        x1_hi = sb("x1_hi", [P, C, G, P], F32R)
        x1_lo = sb("x1_lo", [P, C, G, P], F32R)
        xp_t = sb("xp_t", [P, C, G, P])
        xp = sb("xp", [P, G, D])
        xc_t = sb("xc_t", [P, C, G, P])
        attn = sb("attn", [P, PAIRS, QH, C, 2, P])
        x2 = sb("x2", [P, G, D])
        adj_b = sb("adj_b", [P, G, P])
        x2_hi = sb("x2_hi", [P, C, G, P], F32R)
        x2_lo = sb("x2_lo", [P, C, G, P], F32R)
        qk = sb("qk", [P, G, QK])
        qak = sb("qak", [P, G, E])
        wsum = sb("wsum", [P, G])
        wmax = sb("wmax", [G, 1])
        wbias = sb("wbias", [G, 1])
        wexp = sb("wexp", [G, P])
        wden = sb("wden", [G, 1])
        wrec = sb("wrec", [G, 1])
        wnorm = sb("wnorm", [G, P])
        wcol = sb("wcol", [P, G])
        yb = sb("yb", [P, G, D])
        x3 = sb("x3", [P, G, D])
        x3_hi = sb("x3_hi", [P, C, G, P], F32R)
        x3_lo = sb("x3_lo", [P, C, G, P], F32R)
        s1 = sb("s1", [P, G, D])
        h1_t = sb("h1_t", [P, C, G, P])
        s2 = sb("s2", [P, G, D])
        h2_t = sb("h2_t", [P, C, G, P])
        s3 = sb("s3", [P, G, D])
        yo = sb("yo", [P, G, D])
        x4 = sb("x4", [P, G, D])
        st = [sb(f"st{n}", [P, G, 6]) for n in range(4)]
        mv = [sb(f"mv{n}", [P, G, 2]) for n in range(4)]
        ve = [sb(f"ve{n}", [P, G]) for n in range(4)]
        rs = [sb(f"rs{n}", [P, G]) for n in range(4)]

        ps = ctx.enter_context(nc.psum_tensor("ps", [P, 8, 512], F32))

        def bank(n):
            return ps[:, n, :]

        def half(n, j):
            return ps[:, n, j * D:(j + 1) * D]

        def quarter(n, b):
            return ps[:, n, b * P:(b + 1) * P]

        w_loaded = sem("w_loaded")
        c_zeroed = sem("c_zeroed")
        c_loaded = sem("c_loaded")
        consts = sem("consts")
        ident_ready = sem("ident_ready")
        seed_ready = sem("seed_ready")
        wva_mm = sem("wva_mm")
        wva_sb = sem("wva_sb")
        zb_sb = sem("zb_sb")
        z_const_ready = sem("z_const_ready")
        w_hi_ready = sem("w_hi_ready")
        w_lo_ready = sem("w_lo_ready")
        row_sum = sem("row_sum")
        row_hi_ready = sem("row_hi_ready")
        row_lo_ready = sem("row_lo_ready")
        row_moved = sem("row_moved")
        x_loaded = sem("x_loaded")
        xt_loaded = sem("xt_loaded")
        adj_a_loaded = sem("adj_a_loaded")
        adj_b_loaded = sem("adj_b_loaded")
        stored = sem("stored")
        xa_hi_ready = sem("xa_hi_ready")
        xa_lo_ready = sem("xa_lo_ready")
        y2_mm = sem("y2_mm")
        y2_ready = sem("y2_ready")
        si_mm = sem("si_mm")
        zsum_ready = sem("zsum_ready")
        zrelu_ready = sem("zrelu_ready")
        zexp_ready = sem("zexp_ready")
        alpha_ready = sem("alpha_ready")
        rsum_mm = sem("rsum_mm")
        rrow_ready = sem("rrow_ready")
        rden_ready = sem("rden_ready")
        trans_ready = sem("trans_ready")
        xw0_mm = sem("xw0_mm")
        zed_mm = sem("zed_mm")
        zed_ready = sem("zed_ready")
        h_mm = sem("h_mm")
        x1t_mm = sem("x1t_mm")
        x1_hi_ready = sem("x1_hi_ready")
        x1_lo_ready = sem("x1_lo_ready")
        xpt_mm = sem("xpt_mm")
        xpt_ready = sem("xpt_ready")
        xp_mm = sem("xp_mm")
        xp_ready = sem("xp_ready")
        xct_mm = sem("xct_mm")
        xct_ready = sem("xct_ready")
        score_mm = sem("score_mm")
        score_ready = sem("score_ready")
        attn_ready = sem("attn_ready")
        xh_mm = sem("xh_mm")
        x2t_mm = sem("x2t_mm")
        x2_hi_ready = sem("x2_hi_ready")
        x2_lo_ready = sem("x2_lo_ready")
        qkv_mm = sem("qkv_mm")
        qk_ready = sem("qk_ready")
        ak_mm = sem("ak_mm")
        qak_ready = sem("qak_ready")
        wsum_ready = sem("wsum_ready")
        wt_mm = sem("wt_mm")
        wmax_ready = sem("wmax_ready")
        wbias_ready = sem("wbias_ready")
        wexp_ready = sem("wexp_ready")
        wrec_ready = sem("wrec_ready")
        wnorm_ready = sem("wnorm_ready")
        wcol_mm = sem("wcol_mm")
        wcol_ready = sem("wcol_ready")
        x3t_mm = sem("x3t_mm")
        x3_hi_ready = sem("x3_hi_ready")
        x3_lo_ready = sem("x3_lo_ready")
        s1_mm = sem("s1_mm")
        s1_ready = sem("s1_ready")
        h1_mm = sem("h1_mm")
        h1_ready = sem("h1_ready")
        s2_mm = sem("s2_mm")
        s2_ready = sem("s2_ready")
        h2_mm = sem("h2_mm")
        h2_ready = sem("h2_ready")
        s3_mm = sem("s3_mm")
        s3_ready = sem("s3_ready")
        o_mm = sem("o_mm")
        y_ready = [sem(f"ln{n}_in_ready") for n in range(4)]
        st_ready = [sem(f"ln{n}_st_ready") for n in range(4)]
        mv_ready = [sem(f"ln{n}_mv_ready") for n in range(4)]
        ve_ready = [sem(f"ln{n}_ve_ready") for n in range(4)]
        rs_ready = [sem(f"ln{n}_rs_ready") for n in range(4)]
        x_ready = [sem(f"ln{n}_out_ready") for n in range(4)]

        plain_loads = [(w_raw[:, 0:W_Y2 + C * Y2W].rearrange("p (c w) -> p c w", c=C)[:, :, 0:D],
                        wraw[:, 0:C * D].rearrange("p (c w) -> p c w", c=C)),
                       (w_raw[:, W_Z:W_END], wraw[:, C * D:]),
                       (wv_t[:], wvT), (aw_c[:], awc), (bv_c[:], bvc), (ab_c[:], ab), (bk_row[:], bk),
                       (bp_c[:], bpc), (b1_c[:], b1c), (b2_c[:], b2c), (w_23[:], w23),
                       (rows_raw[:, 1, :], b3)]
        W_LOADS = 16 * len(plain_loads)
        CONSTS = 5

        x_dram = x.rearrange("(i b) n d -> i n b d", b=G)
        out_dram = out.rearrange("(i b) n d -> i n b d", b=G)

        block = ctx.enter_context(nc.Block())

        @block.sync
        def _(sp):
            for dst, src in plain_loads:
                sp.dma_start(dst, src).then_inc(w_loaded, 16)
            sp.wait_ge(c_zeroed, 1)
            for h in range(H):
                r = DH * (h % QH)
                sp.dma_start(c_t[r:r + DH, h // QH, r:r + DH], cT[h]).then_inc(c_loaded, 16)
            sp.wait_ge(row_lo_ready, 1)
            sp.dma_start(rows[1:2].bitcast(F32), row_lo[:].bitcast(F32)).then_inc(row_moved, 16)

            def load(g):
                t = Turn(sp, g)
                t.wait(xa_lo_ready, 1, 0)
                sp.dma_start(xa_t[:], xT[g]).then_inc(xt_loaded, 16)
                t.wait(score_ready, 4, 0)
                sp.dma_start(adj_a[:], aT[g]).then_inc(adj_a_loaded, 16)
                t.wait(y_ready[0], 2, 0)
                sp.dma_start(xa[:], x_dram[g]).then_inc(x_loaded, 16)
                t.wait(o_mm, 2, 0)
                sp.dma_start(adj_b[:], aT[g]).then_inc(adj_b_loaded, 16)

            load(0)
            with sp.Fori(1, GROUPS) as g:
                load(g)

        @block.tensor
        def _(pe):
            def product(dst, left, right, start, stop):
                pe.matmul(dst, left[1], right[0], start=start, stop=False, skip_group_check=True)
                pe.matmul(dst, left[0], right[1], start=False, stop=False, skip_group_check=True)
                return pe.matmul(dst, left[0], right[0], start=False, stop=stop, skip_group_check=True)

            def weights(at, width, c):
                a = at + c * width
                return w_hi[:, a:a + width], w_lo[:, a:a + width]

            def split(hi, lo, c, b):
                return hi[:, c, b, :], lo[:, c, b, :]

            def rows_times(dst, hi, lo, b, at, width, start, stop):
                for c in range(C):
                    mm = product(dst, split(hi, lo, c, b), weights(at, width, c),
                                 start and c == 0, stop and c == C - 1)
                return mm

            def turn_rows(src, first, done):
                for c in range(C):
                    for b in range(G):
                        mm = pe.transpose(quarter(first + c, b), src[:, b, c * P:(c + 1) * P], ident[:])
                    mm.then_inc(done, 1)

            def a_y2(t):
                t.wait(xa_hi_ready, 1)
                t.wait(xa_lo_ready, 1)
                t.wait(y_ready[1], 2, 0)
                for b in range(G):
                    rows_times(ps[:, b, 0:Y2W], xa_hi, xa_lo, b, W_Y2, Y2W, True, True).then_inc(y2_mm, 1)

            def a_xw1(t):
                t.wait(y2_ready, 2)
                for b in range(G):
                    rows_times(half(2 + b // 2, b % 2), xa_hi, xa_lo, b, W_Z, D, b % 2 == 0, False)

            def a_si(t):
                t.wait(y2_ready, 2)
                for b in range(G):
                    mm = pe.transpose(quarter(0, b), y2[:, b, D + 1:D + 2].broadcast_to([P, P]), ident[:])
                mm.then_inc(si_mm, 1)

            def a_rsum(t):
                t.wait(alpha_ready, 1)
                pe.matmul(bank(1), ones[:], alpha[:], start=True, stop=True).then_inc(rsum_mm, 1)

            def a_xw0(t):
                t.wait(rrow_ready, 1)
                for b in range(G):
                    dst = half(b // 2, b % 2)
                    pe.matmul(dst, ones_r[:], rows[:, 0, :], start=(b % 2 == 0), stop=False,
                              skip_group_check=True)
                    mm = rows_times(dst, xa_hi, xa_lo, b, W_H, D, False, False)
                mm.then_inc(xw0_mm, 1)

            def a_ty2(t):
                t.wait(trans_ready, 1)
                for b in range(G):
                    mm = pe.matmul(half(2 + b // 2, b % 2), trans[:, b, :], y2[:, b, 0:D],
                                   start=False, stop=True, skip_group_check=True)
                    if b % 2:
                        mm.then_inc(zed_mm, 1)

            def a_tz(t):
                for p in range(PAIRS):
                    t.wait(zed_ready, 2, p + 1)
                    for j in range(2):
                        b = 2 * p + j
                        mm = pe.matmul(half(p, j), trans[:, b, :], zed[:, b, :],
                                       start=False, stop=True, skip_group_check=True)
                    mm.then_inc(h_mm, 1)

            def a_x1t(t):
                t.wait(x_ready[0], 1)
                turn_rows(x1, 2, x1t_mm)

            def a_xpt(t):
                t.wait(x1_hi_ready, 2)
                t.wait(x1_lo_ready, 2)
                for m in range(C):
                    for c in range(C):
                        w = W_P + c * D + m * P
                        mm = product(bank(m), (w_hi[:, w:w + P], w_lo[:, w:w + P]),
                                     (x1_hi[:, c], x1_lo[:, c]), c == 0, c == C - 1)
                    mm.then_inc(xpt_mm, 1)

            def a_xp(t):
                t.wait(xpt_ready, 2)
                for b in range(G):
                    for c in range(C):
                        mm = pe.transpose(ps[:, 2 + b // 2, (b % 2) * D + c * P:][:, 0:P],
                                          xp_t[:, c, b, :], ident[:])
                    if b % 2:
                        mm.then_inc(xp_mm, 1)

            def a_xct(t):
                for c in range(C):
                    pe.matmul(bank(c), c_t[:, c, :], xp_t[:, c], start=True, stop=True).then_inc(xct_mm, 1)

            def a_scores(t, p):
                if p == 0:
                    t.wait(xct_ready, 2)
                    t.wait(xp_ready, 2)
                else:
                    t.wait(score_ready, 4, 2)
                for c in range(C):
                    for j in range(2):
                        for q in range(QH):
                            rows_q = slice(DH * q, DH * q + DH)
                            mm = pe.matmul(ps[:, q, (2 * c + j) * P:(2 * c + j + 1) * P],
                                           xp_t[rows_q, c, 2 * p + j, :], xc_t[rows_q, c, 2 * p + j, :],
                                           start=True, stop=True)
                mm.then_inc(score_mm, 1)

            def a_xh(t, p):
                t.wait(attn_ready, 4, 2 * p + 2)
                if p == 0:
                    t.wait(score_ready, 4, 4)
                for j in range(2):
                    for h in range(H):
                        mm = pe.matmul(ps[:, p, j * D + h * DH:j * D + (h + 1) * DH],
                                       attn[:, p, h % QH, h // QH, j, :],
                                       xp[:, 2 * p + j, h * DH:(h + 1) * DH], start=True, stop=True)
                mm.then_inc(xh_mm, 1)

            def b_x2t(t):
                t.wait(x_ready[1], 1)
                t.wait(y_ready[3], 2, 0)
                turn_rows(x2, 4, x2t_mm)

            def b_qkv(t):
                t.wait(x2_hi_ready, 2)
                t.wait(x2_lo_ready, 2)
                t.wait(s3_ready, 2, 0)
                for b in range(G):
                    mm = rows_times(ps[:, 4 + b, 0:QKVW], x2_hi, x2_lo, b, W_QKV, QKVW, True, True)
                mm.then_inc(qkv_mm, 1)

            def b_ak(t):
                t.wait(qk_ready, 1)
                t.wait(adj_b_loaded, 16)
                for b in range(G):
                    mm = pe.matmul(ps[:, 4 + b, QKVW:QKVW + E], adj_b[:, b, :], qk[:, b, E:QK],
                                   start=True, stop=True)
                mm.then_inc(ak_mm, 1)

            def b_wt(t):
                t.wait(wsum_ready, 1)
                pe.matmul(ps[0:G, 4, D:D + P], wsum[:], ident[:], start=True, stop=True).then_inc(wt_mm, 1)

            def b_wcol(t):
                t.wait(wnorm_ready, 1)
                pe.matmul(ps[:, 5, D:D + G], wnorm[:], ident[0:G, 0:G], start=True, stop=True)\
                  .then_inc(wcol_mm, 1)

            def b_x3t(t):
                t.wait(x_ready[2], 1)
                turn_rows(x3, 4, x3t_mm)

            def b_s1(t):
                t.wait(x3_hi_ready, 2)
                t.wait(x3_lo_ready, 2)
                for b in range(G):
                    mm = rows_times(half(6 + b // 2, b % 2), x3_hi, x3_lo, b, W_S1, D, True, True)
                    if b % 2:
                        mm.then_inc(s1_mm, 1)

            def gcn_turn(t, s, s_ready, done):
                t.wait(s_ready, 2)
                for c in range(C):
                    for b in range(G):
                        mm = pe.matmul(quarter(4 + c, b), s[:, b, c * P:(c + 1) * P], adj_b[:, b, :],
                                       start=True, stop=True)
                    mm.then_inc(done, 1)

            def gcn_weights(t, h_t, h_ready, n, done):
                t.wait(h_ready, 2)
                for b in range(G):
                    for c in range(C):
                        mm = pe.matmul(half(6 + b // 2, b % 2), h_t[:, c, b, :], w_23[:, n, c, :],
                                       start=(c == 0), stop=(c == C - 1))
                    if b % 2:
                        mm.then_inc(done, 1)

            def b_out(t):
                t.wait(s3_ready, 2)
                for b in range(G):
                    dst = half(4 + b // 2, b % 2)
                    pe.matmul(dst, ones_r[:], rows[:, 1, :], start=True, stop=False)
                    mm = pe.matmul(dst, adj_b[:, b, :], s3[:, b, :], start=False, stop=True)
                    if b % 2:
                        mm.then_inc(o_mm, 1)

            pe.wait_ge(w_loaded, W_LOADS)
            for m in range(C):
                for c in range(C):
                    mm = pe.matmul(ps[:, 0, 2 * m:2 * m + 2], wv_t[:, c, m * P:(m + 1) * P], aw_c[:, :, c],
                                   start=(c == 0), stop=(c == C - 1))
            for c in range(C):
                mm = pe.matmul(ps[:, 1, 0:2], bv_c[:, c:c + 1].broadcast_to([P, P]), aw_c[:, :, c],
                               start=(c == 0), stop=(c == C - 1))
            mm.then_inc(wva_mm, 1)
            pe.wait_ge(w_hi_ready, 2)
            pe.wait_ge(w_lo_ready, 2)
            pe.wait_ge(consts, CONSTS)
            pe.wait_ge(ident_ready, 1)
            pe.wait_ge(row_moved, 16)
            pe.wait_ge(c_loaded, 16 * H)

            def both(a, b):
                if a is not None:
                    a = Turn(pe, a)
                    a_y2(a)
                if b is not None:
                    b = Turn(pe, b)
                    b_x2t(b)
                if a:
                    a_xw1(a)
                    a_si(a)
                if b:
                    b_qkv(b)
                if a:
                    a_rsum(a)
                if b:
                    b_ak(b)
                if a:
                    a_xw0(a)
                    a_ty2(a)
                if b:
                    b_wt(b)
                if a:
                    a_tz(a)
                if b:
                    b_wcol(b)
                if a:
                    a_x1t(a)
                if b:
                    b_x3t(b)
                if a:
                    a_xpt(a)
                if b:
                    b_s1(b)
                if a:
                    a_xp(a)
                    a_xct(a)
                if b:
                    gcn_turn(b, s1, s1_ready, h1_mm)
                if a:
                    a_scores(a, 0)
                if b:
                    gcn_weights(b, h1_t, h1_ready, 0, s2_mm)
                if a:
                    a_scores(a, 1)
                if b:
                    gcn_turn(b, s2, s2_ready, h2_mm)
                if a:
                    a_xh(a, 0)
                if b:
                    gcn_weights(b, h2_t, h2_ready, 1, s3_mm)
                if a:
                    a_xh(a, 1)
                if b:
                    b_out(b)

            both(0, None)
            both(1, 0)
            with pe.Fori(2, GROUPS) as g:
                both(g, g - 1)
            both(None, GROUPS - 1)

        @block.scalar
        def _(act):
            copy, exp, ident_f = ACT.Copy, ACT.Exp, ACT.Identity
            act.wait_ge(seed_ready, 1)
            act.activation(act_seed[:], act_seed[:], exp).then_inc(w_hi_ready, 1)
            act.wait_ge(w_loaded, W_LOADS)
            act.wait_ge(wva_sb, 1)
            act.activation(w_hi[:], w_raw[:], copy).then_inc(w_hi_ready, 1)
            act.wait_ge(row_sum, 2)
            act.activation(rows[0:1], rows_raw[:], copy).then_inc(row_hi_ready, 1)

            def hi_part(dst, src_bank, mm, ready, t):
                for c in range(C):
                    t.wait(mm, 2, c + 1)
                    act.activation(dst[:, c], bank(src_bank + c), copy).then_inc(ready, 1)

            def out_of_psum(dst, src_bank, mm, ready, t):
                for p in range(PAIRS):
                    t.wait(mm, 2, p + 1)
                    act.activation(dst[:, 2 * p:2 * p + 2, :], bank(src_bank + p), copy).then_inc(ready, 1)

            def relu_of(dst, bias, mm, ready, t):
                for c in range(C):
                    t.wait(mm, 2, c + 1)
                    act.activation(dst[:, c], bank(4 + c), ACT.Relu, bias=bias[:, c:c + 1]).then_inc(ready, 1)

            def both(a, b):
                if a is not None:
                    a = Turn(act, a)
                    for p in range(PAIRS):
                        a.wait(y2_mm, 4, 2 * p + 2)
                        act.activation(y2[:, 2 * p:2 * p + 2, :], ps[:, 2 * p:2 * p + 2, 0:Y2W], copy)\
                           .then_inc(y2_ready, 1)
                if b is not None:
                    b = Turn(act, b)
                    hi_part(x2_hi, 4, x2t_mm, x2_hi_ready, b)
                if a:
                    a.wait(zrelu_ready, 1)
                    act.activation(zexp[:], zrelu[:], exp).then_inc(zexp_ready, 1)
                if b:
                    b.wait(qkv_mm, 1)
                    act.activation(qk[:], ps[:, 4:8, D:QKVW], copy).then_inc(qk_ready, 1)
                if a:
                    out_of_psum(zed, 2, zed_mm, zed_ready, a)
                if b:
                    b.wait(wbias_ready, 1)
                    act.activation(wexp[:], ps[0:G, 4, D:D + P], exp, bias=wbias[:], scale=E ** -0.5,
                                   accum_out=wden[:]).then_inc(wexp_ready, 1)
                if a:
                    hi_part(x1_hi, 2, x1t_mm, x1_hi_ready, a)
                if b:
                    hi_part(x3_hi, 4, x3t_mm, x3_hi_ready, b)
                if a:
                    for m in range(C):
                        a.wait(xpt_mm, 2, m + 1)
                        act.activation(xp_t[:, m], bank(m), ident_f, bias=bp_c[:, m:m + 1])\
                           .then_inc(xpt_ready, 1)
                if b:
                    out_of_psum(s1, 6, s1_mm, s1_ready, b)
                if a:
                    for c in range(C):
                        a.wait(xct_mm, 2, c + 1)
                        act.activation(xc_t[:, c], bank(c), copy).then_inc(xct_ready, 1)
                if b:
                    relu_of(h1_t, b1_c, h1_mm, h1_ready, b)

                def tanh(p):
                    for k in range(2):
                        q = slice(2 * k, 2 * k + 2)
                        a.wait(score_ready, 4, 2 * p + k + 1)
                        act.activation(attn[:, p, q], attn[:, p, q], ACT.Tanh).then_inc(attn_ready, 1)

                if a:
                    tanh(0)
                if b:
                    out_of_psum(s2, 6, s2_mm, s2_ready, b)
                if a:
                    tanh(1)
                if b:
                    relu_of(h2_t, b2_c, h2_mm, h2_ready, b)
                    out_of_psum(s3, 6, s3_mm, s3_ready, b)
                    b.wait(x_ready[3], 1)
                    act.dma_start(out_dram[b.group], x4[:]).then_inc(stored, 16)

            both(0, None)
            both(1, 0)
            with act.Fori(2, GROUPS) as g:
                both(g, g - 1)
            both(None, GROUPS - 1)
            act.wait_ge(stored, 16 * GROUPS)

        @block.vector
        def _(dve):
            dve.wait_ge(wva_mm, 1)
            for m in range(C):
                a = W_Y2 + m * Y2W + D
                cp = dve.tensor_copy(w_raw[:, a:a + 2], ps[:, 0, 2 * m:2 * m + 2])
            cp.then_inc(wva_sb, 1)
            dve.tensor_copy(z_bias[:], ps[:, 1, 0:2]).then_inc(zb_sb, 1)
            dve.tensor_tensor(rows_raw[:, 0, :], bk_row[:, 0, :], bk_row[:, 1, :], ALU.add).then_inc(row_sum, 1)
            dve.wait_ge(zb_sb, 1)
            dve.scalar_tensor_tensor(z_const[:], z_bias[:, 0:1], ab_c[:, 0:1], z_bias[:, 1:2],
                                     ALU.add, ALU.add).then_inc(z_const_ready, 1)
            dve.wait_ge(row_sum, 1)
            dve.tensor_tensor(rows_raw[:, 0, :], rows_raw[:, 0, :], bk_row[:, 2, :], ALU.add).then_inc(row_sum, 1)
            dve.wait_ge(w_hi_ready, 2)
            dve.tensor_tensor(w_lo[:], w_raw[:], w_hi[:].bitcast(F32), ALU.subtract).then_inc(w_lo_ready, 2)
            dve.wait_ge(row_hi_ready, 1)
            dve.tensor_tensor(row_lo[:], rows_raw[:], rows[0:1].bitcast(F32), ALU.subtract)\
               .then_inc(row_lo_ready, 1)
            dve.wait_ge(z_const_ready, 1)

            def lo_part(dst, hi, src_bank, hi_ready, ready, t):
                for c in range(C):
                    t.wait(hi_ready, 2, c + 1)
                    dve.tensor_tensor(dst[:, c], bank(src_bank + c), hi[:, c].bitcast(F32), ALU.subtract)\
                       .then_inc(ready, 1)

            def norm_stats(n, y, t):
                t.wait(y_ready[n], 2)
                for b in range(G):
                    op = dve.bn_stats(st[n][:, b, :], y[:, b, :])
                op.then_inc(st_ready[n], 1)
                t.wait(st_ready[n], 1)
                dve.memset(anchor[:, n:n + 1], 0.0)
                for b in range(G):
                    op = dve.bn_aggr(mv[n][:, b, :], st[n][:, b, :])
                op.then_inc(mv_ready[n], 1)
                t.wait(mv_ready[n], 1)
                dve.tensor_scalar(ve[n][:], mv[n][:, :, 1], EPS, None, ALU.add).then_inc(ve_ready[n], 1)

            def norm_rows(n, y, dst, t):
                t.wait(rs_ready[n], 1)
                for b in range(G):
                    op = dve.tensor_scalar(dst[:, b, :], y[:, b, :], mv[n][:, b, 0:1], rs[n][:, b:b + 1],
                                           ALU.subtract, ALU.mult)
                op.then_inc(x_ready[n], 1)

            def sum_relu(n, dst, mm, x_in, t):
                for p in range(PAIRS):
                    t.wait(mm, 2, p + 1)
                    pair = slice(2 * p, 2 * p + 2)
                    dve.scalar_tensor_tensor(dst[:, pair, :], bank(p), 0.0, x_in[:, pair, :],
                                             ALU.max, ALU.add).then_inc(y_ready[n], 1)

            def scores(p, t):
                t.wait(score_mm, 2, p + 1)
                for k in range(2):
                    pair = adj_a[:, 2 * p:2 * p + 2, :].rearrange("p b n -> p (b n)")
                    dve.tensor_tensor(
                        attn[:, p, 2 * k:2 * k + 2].rearrange("p q c b n -> p (q c) (b n)"),
                        ps[:, 2 * k:2 * k + 2, :].rearrange("p q (c m) -> p (q c) m", c=C),
                        pair.unsqueeze(1).broadcast_to([P, 2 * C, 2 * P]), ALU.mult).then_inc(score_ready, 1)

            def both(a, b):
                if b is not None:
                    b = Turn(dve, b)
                    lo_part(x2_lo, x2_hi, 4, x2_hi_ready, x2_lo_ready, b)
                if a is not None:
                    a = Turn(dve, a)
                    a.wait(si_mm, 1)
                    dve.scalar_tensor_tensor(zsum[:], bank(0).rearrange("p (b n) -> p b n", b=G), z_const[:, 0:1],
                                             y2[:, :, D:D + 1].broadcast_to([P, G, P]),
                                             ALU.add, ALU.add).then_inc(zsum_ready, 1)
                    a.wait(zsum_ready, 1)
                    dve.scalar_tensor_tensor(zrelu[:], zsum[:], SLOPE, zsum[:], ALU.mult, ALU.max)\
                       .then_inc(zrelu_ready, 1)
                    a.wait(rsum_mm, 1)
                    dve.tensor_scalar(rrow[:], bank(1), TINY, None, ALU.add).then_inc(rrow_ready, 1)
                    a.wait(rrow_ready, 1)
                    dve.reciprocal(rden[:], rrow[:]).then_inc(rden_ready, 1)
                if b:
                    b.wait(ak_mm, 1)
                    dve.tensor_tensor(qak[:], qk[:, :, 0:E], ps[:, 4:8, QKVW:QKVW + E], ALU.mult)\
                       .then_inc(qak_ready, 1)
                    b.wait(qak_ready, 1)
                    dve.reduce_sum(wsum[:], qak[:], AX_X).then_inc(wsum_ready, 1)
                    b.wait(wt_mm, 1)
                    dve.reduce_max(wmax[:], ps[0:G, 4, D:D + P], AX_X).then_inc(wmax_ready, 1)
                    b.wait(wmax_ready, 1)
                    dve.tensor_scalar(wbias[:], wmax[:], -E ** -0.5, None, ALU.mult).then_inc(wbias_ready, 1)
                    b.wait(wexp_ready, 1)
                    dve.reciprocal(wrec[:], wden[:]).then_inc(wrec_ready, 1)
                    b.wait(wrec_ready, 1)
                    dve.tensor_scalar(wnorm[:], wexp[:], wrec[:, 0:1], None, ALU.mult).then_inc(wnorm_ready, 1)
                if a:
                    a.wait(x_loaded, 16)
                    sum_relu(0, ya, h_mm, xa, a)
                if b:
                    b.wait(wcol_mm, 1)
                    dve.tensor_copy(wcol[:], ps[:, 5, D:D + G]).then_inc(wcol_ready, 1)
                if a:
                    norm_stats(0, ya, a)
                if b:
                    b.wait(wcol_ready, 1)
                    for i in range(G):
                        op = dve.scalar_tensor_tensor(yb[:, i, :], ps[:, 4 + i, 0:D], wcol[:, i:i + 1],
                                                      x2[:, i, :], ALU.mult, ALU.add)
                        if i % 2:
                            op.then_inc(y_ready[2], 1)
                    norm_stats(2, yb, b)
                if a:
                    norm_rows(0, ya, x1, a)
                if b:
                    norm_rows(2, yb, x3, b)
                if a:
                    lo_part(x1_lo, x1_hi, 2, x1_hi_ready, x1_lo_ready, a)
                if b:
                    lo_part(x3_lo, x3_hi, 4, x3_hi_ready, x3_lo_ready, b)
                if a:
                    for p in range(PAIRS):
                        a.wait(xp_mm, 2, p + 1)
                        dve.tensor_copy(xp[:, 2 * p:2 * p + 2, :], bank(2 + p)).then_inc(xp_ready, 1)
                    scores(0, a)
                    scores(1, a)
                    sum_relu(1, ya, xh_mm, x1, a)
                    norm_stats(1, ya, a)
                if b:
                    for p in range(PAIRS):
                        b.wait(o_mm, 2, p + 1)
                        pair = slice(2 * p, 2 * p + 2)
                        dve.tensor_tensor(yo[:, pair, :], bank(4 + p), x3[:, pair, :], ALU.add)\
                           .then_inc(y_ready[3], 1)
                if a:
                    norm_rows(1, ya, x2, a)
                if b:
                    norm_stats(3, yo, b)
                    b.wait(stored, 16, 0)
                    norm_rows(3, yo, x4, b)

            both(0, None)
            both(1, 0)
            with dve.Fori(2, GROUPS) as g:
                both(g, g - 1)
            both(None, GROUPS - 1)

        @block.gpsimd
        def _(pool):
            pool.memset(c_t[:], 0.0).then_inc(c_zeroed, 1)
            pool.memset(act_seed[:], 0.0).then_inc(seed_ready, 1)
            pool.memset(ident[:], 0.0).then_inc(consts, 1)
            pool.memset(ones[:], 1.0).then_inc(consts, 1)
            pool.memset(neg_half[:], -0.5).then_inc(consts, 1)
            pool.wait_ge(consts, 3)
            pool.affine_select(out=ident[:], in_=ident[:], compare_op=ALU.not_equal, fill=1.0, base=0,
                               pattern=[[-1, P]], channel_multiplier=1).then_inc(ident_ready, 1)
            pool.tensor_copy(ones_r[:], ones[0:2, :]).then_inc(consts, 2)

            def split_x(g):
                t = Turn(pool, g)
                t.wait(xw0_mm, 1, 0)
                t.wait(xt_loaded, 16)
                one = ones[:, 0:1].unsqueeze(1).unsqueeze(1).broadcast_to([P, C, G, P])
                pool.tensor_tensor(xa_hi[:], xa_t[:], one, ALU.mult).then_inc(xa_hi_ready, 1)
                t.wait(xa_hi_ready, 1)
                pool.tensor_tensor(xa_lo[:], xa_t[:], xa_hi[:].bitcast(F32), ALU.subtract)\
                    .then_inc(xa_lo_ready, 1)

            def a_alpha(t):
                t.wait(adj_a_loaded, 16)
                t.wait(zexp_ready, 1)
                pool.tensor_tensor(alpha[:], adj_a[:], zexp[:], ALU.mult).then_inc(alpha_ready, 1)

            def a_trans(t):
                t.wait(rden_ready, 1)
                pool.tensor_tensor(trans[:], alpha[:], rden[:], ALU.mult).then_inc(trans_ready, 1)

            def norm_scale(n, t):
                t.wait(ve_ready[n], 1)
                pool.tensor_tensor(rs[n][:], ve[n][:], neg_half[:], ALU.pow).then_inc(rs_ready[n], 1)

            def both(a, b):
                if a is not None:
                    a = Turn(pool, a)
                    a_alpha(a)
                    a_trans(a)
                    norm_scale(0, a)
                if b is not None:
                    b = Turn(pool, b)
                    norm_scale(2, b)
                if a and not (isinstance(a.group, int) and a.group == GROUPS - 1):
                    split_x(a.group + 1)
                if a:
                    norm_scale(1, a)
                if b:
                    norm_scale(3, b)

            split_x(0)
            both(0, None)
            both(1, 0)
            with pool.Fori(2, GROUPS - 1) as g:
                both(g, g - 1)
            both(GROUPS - 1, GROUPS - 2)
            both(None, GROUPS - 1)


_OUT = (B, P, D)


def kernel(x, adj, L0_gnn_Wv, L0_gnn_bv, L0_gnn_aw, L0_gnn_ab, L0_gnn_Wk, L0_gnn_bk, L1_gnn_Wp, L1_gnn_bp,
           L1_gnn_C, L2_gnn_W_qk, L2_gnn_W_v, L3_gnn_W1, L3_gnn_b1, L3_gnn_W2, L3_gnn_b2, L3_gnn_W3, L3_gnn_b3):
    import numpy as np
    import concourse.bacc as bacc
    from concourse.bass_utils import run_bass_kernel_spmd

    def lay(a, shape, order):
        return np.ascontiguousarray(np.asarray(a).reshape(shape).transpose(order))

    def chunks(w):
        w = np.asarray(w)
        return lay(w, (C, P, w.shape[1]), (1, 0, 2))

    wk, qk = np.asarray(L0_gnn_Wk), np.asarray(L2_gnn_W_qk)
    wp = lay(L1_gnn_Wp, (H, D, DH), (1, 0, 2)).reshape(D, D)
    qkv = np.concatenate([np.asarray(L2_gnn_W_v), qk]).T
    wraw = np.concatenate([chunks(w).reshape(P, -1) for w in (wk[2], wk[1], wk[0], wp, qkv, L3_gnn_W1)], axis=1)
    arrays = {
        "x": np.ascontiguousarray(np.asarray(x)),
        "xT": lay(x, (GROUPS, G, P, C, P), (0, 4, 3, 1, 2)),
        "aT": lay(adj, (GROUPS, G, P, P), (0, 3, 1, 2)),
        "wraw": np.ascontiguousarray(wraw),
        "wvT": chunks(np.asarray(L0_gnn_Wv).T),
        "awc": lay(L0_gnn_aw, (2, C, P), (2, 0, 1)),
        "bvc": lay(L0_gnn_bv, (C, P), (1, 0)),
        "ab": np.ascontiguousarray(np.broadcast_to(np.asarray(L0_gnn_ab).reshape(1, 1), (P, 1))),
        "bk": lay(L0_gnn_bk, (1, 3, D), (0, 1, 2)),
        "bpc": lay(L1_gnn_bp, (C, P), (1, 0)),
        "cT": lay(L1_gnn_C, (H, DH, DH), (0, 2, 1)),
        "b1c": lay(L3_gnn_b1, (C, P), (1, 0)),
        "b2c": lay(L3_gnn_b2, (C, P), (1, 0)),
        "w23": np.ascontiguousarray(np.stack([chunks(L3_gnn_W2), chunks(L3_gnn_W3)], axis=1)),
        "b3": lay(L3_gnn_b3, (1, D), (0, 1)),
    }
    nc = bacc.Bacc("TRN2", target_bir_lowering=False, num_devices=1)
    args = [nc.dram_tensor(f"in_{n}", a.shape, mybir.dt.from_np(a.dtype), kind="ExternalInput").ap()
            for n, a in arrays.items()]
    args.append(nc.dram_tensor("out", _OUT, F32, kind="ExternalOutput").ap())
    build(nc, *args)
    r = run_bass_kernel_spmd(nc, [{f"in_{n}": a for n, a in arrays.items()}], core_ids=[0])
    return r.results[0]["out"]
```

```python
from contextlib import ExitStack

import concourse.bass as bass
from concourse import mybir

F32 = mybir.dt.float32
F32R = mybir.dt.float32r
ALU = mybir.AluOpType
ACT = mybir.ActivationFunctionType
AX_X = mybir.AxisListType.X

P = 128
B = 64
D = 256
C = D // P
G = 4
GROUPS = B // G
PAIRS = G // 2
H = 8
DH = D // H
QH = P // DH
E = 64
QK = 2 * E
EPS = 1e-5
TINY = 1e-12
SLOPE = 0.2

W_Y2, Y2W = 0, D + 2
W_Z = W_Y2 + C * Y2W
W_H = W_Z + C * D
W_P = W_H + C * D
W_QKV, QKVW = W_P + C * D, D + QK
W_S1 = W_QKV + C * QKVW
W_END = W_S1 + C * D


class Turn:

    def __init__(self, engine, group):
        self.engine, self.group, self.known = engine, group, {}

    def wait(self, semaphore, each, k=None):
        k = each if k is None else k
        if isinstance(self.group, int):
            value = self.group * each + k
            if value > 0:
                self.engine.wait_ge(semaphore, value)
            return
        if (each, k) not in self.known:
            self.known[each, k] = self.engine.snap(self.group * each + k)
        self.engine.wait_ge(semaphore, self.known[each, k])


def build(nc, x, xT, aT, wraw, wvT, awc, bvc, ab, bk, bpc, cT, b1c, b2c, w23, b3, out):
    with ExitStack() as ctx:
        def sb(name, shape, dt=F32):
            return ctx.enter_context(nc.sbuf_tensor(name, shape, dt))

        def sem(name):
            return ctx.enter_context(nc.semaphore(name))

        w_raw = sb("w_raw", [P, W_END])
        w_hi = sb("w_hi", [P, W_END], F32R)
        w_lo = sb("w_lo", [P, W_END], F32R)
        wv_t = sb("wv_t", [P, C, D])
        aw_c = sb("aw_c", [P, 2, C])
        bv_c = sb("bv_c", [P, C])
        ab_c = sb("ab_c", [P, 1])
        z_bias = sb("z_bias", [P, 2])
        z_const = sb("z_const", [P, 1])
        bk_row = sb("bk_row", [1, 3, D])
        row_raw = sb("row_raw", [1, D])
        row = sb("row", [2, D], F32R)
        row_lo = sb("row_lo", [1, D], F32R)
        b3_rows = sb("b3_rows", [P, D])
        bp_c = sb("bp_c", [P, C])
        b1_c = sb("b1_c", [P, C])
        b2_c = sb("b2_c", [P, C])
        c_t = sb("c_t", [P, C, P])
        w_23 = sb("w_23", [P, 2, C, D])
        ident = sb("ident", [P, P])
        ones = sb("ones", [P, P])
        ones_r = sb("ones_r", [2, P], F32R)
        neg_half = sb("neg_half", [P, G])
        anchor = sb("anchor", [1, 4])
        act_seed = sb("act_seed", [P, 1])
        xa = sb("xa", [P, G, D])
        xa_t = sb("xa_t", [P, C, G, P])
        xa_hi = sb("xa_hi", [P, C, G, P], F32R)
        xa_lo = sb("xa_lo", [P, C, G, P], F32R)
        adj_a = sb("adj_a", [P, G, P])
        y2 = sb("y2", [P, G, Y2W])
        zsum = sb("zsum", [P, G, P])
        zrelu = sb("zrelu", [P, G, P])
        zexp = sb("zexp", [P, G, P])
        alpha = sb("alpha", [P, G, P])
        rsum = sb("rsum", [P, G])
        rrec = sb("rrec", [P, G])
        trans = sb("trans", [P, G, P])
        zed = sb("zed", [P, G, D])
        ya = sb("ya", [P, G, D])
        x1 = sb("x1", [P, G, D])
        x1_hi = sb("x1_hi", [P, C, G, P], F32R)
        x1_lo = sb("x1_lo", [P, C, G, P], F32R)
        xp_t = sb("xp_t", [P, C, G, P])
        xp = sb("xp", [P, G, D])
        xc_t = sb("xc_t", [P, C, G, P])
        attn = sb("attn", [P, PAIRS, QH, C, 2, P])
        x2 = sb("x2", [P, G, D])
        x2_kept = sb("x2_kept", [P, G, D])
        x3 = sb("x3", [P, G, D])
        adj_b = sb("adj_b", [P, G, P])
        x2_hi = sb("x2_hi", [P, C, G, P], F32R)
        x2_lo = sb("x2_lo", [P, C, G, P], F32R)
        qk = sb("qk", [P, G, QK])
        qak = sb("qak", [P, G, E])
        wsum = sb("wsum", [P, G])
        wmax = sb("wmax", [G, 1])
        wbias = sb("wbias", [G, 1])
        wexp = sb("wexp", [G, P])
        wden = sb("wden", [G, 1])
        wrec = sb("wrec", [G, 1])
        wnorm = sb("wnorm", [G, P])
        wcol = sb("wcol", [P, G])
        yb = sb("yb", [P, G, D])
        x3b = sb("x3b", [P, G, D])
        x3_hi = sb("x3_hi", [P, C, G, P], F32R)
        x3_lo = sb("x3_lo", [P, C, G, P], F32R)
        s1 = sb("s1", [P, G, D])
        h1_t = sb("h1_t", [P, C, G, P])
        s2 = sb("s2", [P, G, D])
        h2_t = sb("h2_t", [P, C, G, P])
        s3 = sb("s3", [P, G, D])
        yo = sb("yo", [P, G, D])
        x4 = sb("x4", [P, G, D])
        st = [sb(f"st{n}", [P, G, 6]) for n in range(4)]
        mv = [sb(f"mv{n}", [P, G, 2]) for n in range(4)]
        ve = [sb(f"ve{n}", [P, G]) for n in range(4)]
        rs = [sb(f"rs{n}", [P, G]) for n in range(4)]

        ps = ctx.enter_context(nc.psum_tensor("ps", [P, 8, 512], F32))

        def bank(n):
            return ps[:, n, :]

        def half(n, j):
            return ps[:, n, j * D:(j + 1) * D]

        def quarter(n, b):
            return ps[:, n, b * P:(b + 1) * P]

        w_loaded = sem("w_loaded")
        c_zeroed = sem("c_zeroed")
        c_loaded = sem("c_loaded")
        consts = sem("consts")
        ident_ready = sem("ident_ready")
        seed_ready = sem("seed_ready")
        wva_mm = sem("wva_mm")
        wva_sb = sem("wva_sb")
        zb_sb = sem("zb_sb")
        z_const_ready = sem("z_const_ready")
        w_hi_ready = sem("w_hi_ready")
        w_lo_ready = sem("w_lo_ready")
        row_sum = sem("row_sum")
        row_hi_ready = sem("row_hi_ready")
        row_lo_ready = sem("row_lo_ready")
        row_moved = sem("row_moved")
        x_loaded = sem("x_loaded")
        xt_loaded = sem("xt_loaded")
        adj_a_loaded = sem("adj_a_loaded")
        adj_b_loaded = sem("adj_b_loaded")
        stored = sem("stored")
        xa_hi_ready = sem("xa_hi_ready")
        xa_lo_ready = sem("xa_lo_ready")
        y2_mm = sem("y2_mm")
        y2_ready = sem("y2_ready")
        si_mm = sem("si_mm")
        zsum_ready = sem("zsum_ready")
        zrelu_ready = sem("zrelu_ready")
        zexp_ready = sem("zexp_ready")
        alpha_ready = sem("alpha_ready")
        rsum_mm = sem("rsum_mm")
        rsum_ready = sem("rsum_ready")
        rrec_ready = sem("rrec_ready")
        rt_mm = sem("rt_mm")
        trans_ready = sem("trans_ready")
        xw0_mm = sem("xw0_mm")
        zed_mm = sem("zed_mm")
        zed_ready = sem("zed_ready")
        h_mm = sem("h_mm")
        x1t_mm = sem("x1t_mm")
        x1_hi_ready = sem("x1_hi_ready")
        x1_lo_ready = sem("x1_lo_ready")
        xpt_mm = sem("xpt_mm")
        xpt_ready = sem("xpt_ready")
        xp_mm = sem("xp_mm")
        xp_ready = sem("xp_ready")
        xct_mm = sem("xct_mm")
        xct_ready = sem("xct_ready")
        score_mm = sem("score_mm")
        score_ready = sem("score_ready")
        attn_ready = sem("attn_ready")
        xh_mm = sem("xh_mm")
        x2t_mm = sem("x2t_mm")
        x2_hi_ready = sem("x2_hi_ready")
        x2_lo_ready = sem("x2_lo_ready")
        x2_kept_ready = sem("x2_kept_ready")
        qkv_mm = sem("qkv_mm")
        qk_ready = sem("qk_ready")
        ak_mm = sem("ak_mm")
        qak_ready = sem("qak_ready")
        wsum_ready = sem("wsum_ready")
        wt_mm = sem("wt_mm")
        wmax_ready = sem("wmax_ready")
        wbias_ready = sem("wbias_ready")
        wexp_ready = sem("wexp_ready")
        wrec_ready = sem("wrec_ready")
        wnorm_ready = sem("wnorm_ready")
        wcol_mm = sem("wcol_mm")
        wcol_ready = sem("wcol_ready")
        x3b_ready = sem("x3b_ready")
        x3t_mm = sem("x3t_mm")
        x3_hi_ready = sem("x3_hi_ready")
        x3_lo_ready = sem("x3_lo_ready")
        s1_mm = sem("s1_mm")
        s1_ready = sem("s1_ready")
        h1_mm = sem("h1_mm")
        h1_ready = sem("h1_ready")
        s2_mm = sem("s2_mm")
        s2_ready = sem("s2_ready")
        h2_mm = sem("h2_mm")
        h2_ready = sem("h2_ready")
        s3_mm = sem("s3_mm")
        s3_ready = sem("s3_ready")
        o_mm = sem("o_mm")
        y_ready = [sem(f"ln{n}_in_ready") for n in range(4)]
        st_ready = [sem(f"ln{n}_st_ready") for n in range(4)]
        mv_ready = [sem(f"ln{n}_mv_ready") for n in range(4)]
        ve_ready = [sem(f"ln{n}_ve_ready") for n in range(4)]
        rs_ready = [sem(f"ln{n}_rs_ready") for n in range(4)]
        x_ready = [sem(f"ln{n}_out_ready") for n in range(4)]

        plain_loads = [(w_raw[:, 0:W_Y2 + C * Y2W].rearrange("p (c w) -> p c w", c=C)[:, :, 0:D],
                        wraw[:, 0:C * D].rearrange("p (c w) -> p c w", c=C)),
                       (w_raw[:, W_Z:W_END], wraw[:, C * D:]),
                       (wv_t[:], wvT), (aw_c[:], awc), (bv_c[:], bvc), (ab_c[:], ab), (bk_row[:], bk),
                       (bp_c[:], bpc), (b1_c[:], b1c), (b2_c[:], b2c), (w_23[:], w23),
                       (b3_rows[:], b3)]
        W_LOADS = 16 * len(plain_loads)
        CONSTS = 5

        x_dram = x.rearrange("(i b) n d -> i n b d", b=G)
        out_dram = out.rearrange("(i b) n d -> i n b d", b=G)

        block = ctx.enter_context(nc.Block())

        @block.sync
        def _(sp):
            for dst, src in plain_loads:
                sp.dma_start(dst, src).then_inc(w_loaded, 16)
            sp.wait_ge(c_zeroed, 1)
            for h in range(H):
                r = DH * (h % QH)
                sp.dma_start(c_t[r:r + DH, h // QH, r:r + DH], cT[h]).then_inc(c_loaded, 16)
            sp.wait_ge(row_lo_ready, 1)
            sp.dma_start(row[1:2].bitcast(F32), row_lo[:].bitcast(F32)).then_inc(row_moved, 16)

            def load_xt(g):
                t = Turn(sp, g)
                t.wait(xa_lo_ready, 1, 0)
                sp.dma_start(xa_t[:], xT[g]).then_inc(xt_loaded, 16)

            def load_x(g):
                t = Turn(sp, g)
                t.wait(y_ready[0], 2, 0)
                sp.dma_start(xa[:], x_dram[g]).then_inc(x_loaded, 16)

            def load_adj_a(g):
                t = Turn(sp, g)
                t.wait(score_ready, 4, 0)
                sp.dma_start(adj_a[:], aT[g]).then_inc(adj_a_loaded, 16)

            def load_adj_b(g):
                t = Turn(sp, g)
                t.wait(o_mm, 2, 0)
                sp.dma_start(adj_b[:], aT[g]).then_inc(adj_b_loaded, 16)

            def store(g):
                t = Turn(sp, g)
                t.wait(x_ready[3], 2)
                sp.dma_start(out_dram[g], x4[:]).then_inc(stored, 16)

            def body(g, more=True, b=True, c=True):
                if more:
                    load_xt(g + 1)
                    load_x(g + 1)
                if b:
                    load_adj_b(g - 1)
                if c:
                    store(g - 2)
                if more:
                    load_adj_a(g + 1)

            load_xt(0)
            load_x(0)
            load_adj_a(0)
            body(0, b=False, c=False)
            body(1, c=False)
            body(2)
            with sp.Fori(3, GROUPS - 1) as g:
                body(g)
            body(GROUPS - 1, more=False)
            body(GROUPS, more=False)
            body(GROUPS + 1, more=False, b=False)
            sp.wait_ge(stored, 16 * GROUPS)

        @block.tensor
        def _(pe):
            def product(dst, left, right, start, stop):
                pe.matmul(dst, left[1], right[0], start=start, stop=False, skip_group_check=True)
                pe.matmul(dst, left[0], right[1], start=False, stop=False, skip_group_check=True)
                return pe.matmul(dst, left[0], right[0], start=False, stop=stop, skip_group_check=True)

            def weights(at, width, c):
                a = at + c * width
                return w_hi[:, a:a + width], w_lo[:, a:a + width]

            def split(hi, lo, c, b):
                return hi[:, c, b, :], lo[:, c, b, :]

            def rows_times(dst, hi, lo, b, at, width, start, stop):
                for c in range(C):
                    mm = product(dst, split(hi, lo, c, b), weights(at, width, c),
                                 start and c == 0, stop and c == C - 1)
                return mm

            def turn_rows(t, src, n, first, done):
                for p in range(PAIRS):
                    t.wait(x_ready[n], 2, p + 1)
                    for c in range(C):
                        for b in (2 * p, 2 * p + 1):
                            mm = pe.transpose(quarter(first + c, b), src[:, b, c * P:(c + 1) * P], ident[:])
                        if p == PAIRS - 1:
                            mm.then_inc(done, 1)

            def a_y2(t, p):
                t.wait(xa_hi_ready, 1)
                t.wait(xa_lo_ready, 1)
                t.wait(y_ready[1], 2, 0)
                for b in (2 * p, 2 * p + 1):
                    mm = rows_times(ps[:, b, 0:Y2W], xa_hi, xa_lo, b, W_Y2, Y2W, True, True)
                mm.then_inc(y2_mm, 1)

            def a_xw1(t, b):
                t.wait(y2_ready, 2)
                rows_times(half(2 + b // 2, b % 2), xa_hi, xa_lo, b, W_Z, D, b % 2 == 0, False)

            def a_si(t):
                t.wait(y2_ready, 2)
                for b in range(G):
                    mm = pe.transpose(quarter(0, b), y2[:, b, D + 1:D + 2].broadcast_to([P, P]), ident[:])
                mm.then_inc(si_mm, 1)

            def a_rsum(t):
                t.wait(alpha_ready, 1)
                for b in range(G):
                    mm = pe.matmul(ps[:, 1, b:b + 1], alpha[:, b, :], ones[:, 0:1], start=True, stop=True)
                mm.then_inc(rsum_mm, 1)

            def a_rt(t):
                t.wait(rrec_ready, 1)
                for b in range(G):
                    mm = pe.transpose(quarter(1, b), rrec[:, b:b + 1].broadcast_to([P, P]), ident[:])
                mm.then_inc(rt_mm, 1)

            def a_xw0(t, b):
                t.wait(zsum_ready, 1)
                if b == 2:
                    t.wait(trans_ready, 1)
                dst = half(b // 2, b % 2)
                pe.matmul(dst, ones_r[:], row[:], start=(b % 2 == 0), stop=False, skip_group_check=True)
                mm = rows_times(dst, xa_hi, xa_lo, b, W_H, D, False, False)
                if b == G - 1:
                    mm.then_inc(xw0_mm, 1)

            def a_ty2(t):
                t.wait(trans_ready, 1)
                for b in range(G):
                    mm = pe.matmul(half(2 + b // 2, b % 2), trans[:, b, :], y2[:, b, 0:D],
                                   start=False, stop=True, skip_group_check=True)
                    if b % 2:
                        mm.then_inc(zed_mm, 1)

            def a_tz(t):
                for p in range(PAIRS):
                    t.wait(zed_ready, 2, p + 1)
                    for j in range(2):
                        b = 2 * p + j
                        mm = pe.matmul(half(p, j), trans[:, b, :], zed[:, b, :],
                                       start=False, stop=True, skip_group_check=True)
                    mm.then_inc(h_mm, 1)

            def a_x1t(t):
                turn_rows(t, x1, 0, 2, x1t_mm)

            def a_xpt(t):
                t.wait(x1_hi_ready, 2)
                t.wait(x1_lo_ready, 2)
                for m in range(C):
                    for c in range(C):
                        w = W_P + c * D + m * P
                        mm = product(bank(m), (w_hi[:, w:w + P], w_lo[:, w:w + P]),
                                     (x1_hi[:, c], x1_lo[:, c]), c == 0, c == C - 1)
                    mm.then_inc(xpt_mm, 1)

            def a_xp(t):
                t.wait(xpt_ready, 2)
                for b in range(G):
                    for c in range(C):
                        mm = pe.transpose(ps[:, 2 + b // 2, (b % 2) * D + c * P:][:, 0:P],
                                          xp_t[:, c, b, :], ident[:])
                    if b % 2:
                        mm.then_inc(xp_mm, 1)

            def a_xct(t):
                t.wait(xpt_ready, 2)
                for c in range(C):
                    pe.matmul(bank(c), c_t[:, c, :], xp_t[:, c], start=True, stop=True).then_inc(xct_mm, 1)

            def a_scores(t, p, k):
                if p == 0:
                    t.wait(xct_ready, 2)
                    t.wait(xp_ready, 2)
                else:
                    t.wait(score_ready, 4, k + 1)
                for c in range(C):
                    for j in range(2):
                        for q in (2 * k, 2 * k + 1):
                            rows_q = slice(DH * q, DH * q + DH)
                            mm = pe.matmul(ps[:, q, (2 * c + j) * P:(2 * c + j + 1) * P],
                                           xp_t[rows_q, c, 2 * p + j, :], xc_t[rows_q, c, 2 * p + j, :],
                                           start=True, stop=True)
                mm.then_inc(score_mm, 1)

            def a_xh(t, b):
                p, j = b // 2, b % 2
                t.wait(attn_ready, 4, 2 * p + 2)
                if b == 0:
                    t.wait(score_ready, 4, 3)
                for h in range(H):
                    mm = pe.matmul(ps[:, p, j * D + h * DH:j * D + (h + 1) * DH],
                                   attn[:, p, h % QH, h // QH, j, :],
                                   xp[:, b, h * DH:(h + 1) * DH], start=True, stop=True)
                if j:
                    mm.then_inc(xh_mm, 1)

            def b_x2t(t, bank_free):
                if bank_free:
                    bank_free.wait(h2_ready, 2)
                turn_rows(t, x2, 1, 4, x2t_mm)

            def b_qkv(t, b, bank_free):
                t.wait(x2_hi_ready, 2)
                t.wait(x2_lo_ready, 2)
                if b >= 2 and bank_free:
                    bank_free.wait(y_ready[3], 2)
                rows_times(ps[:, 4 + b, 0:QKVW], x2_hi, x2_lo, b, W_QKV, QKVW, True, True).then_inc(qkv_mm, 1)

            def c_ak(t):
                t.wait(qk_ready, 1)
                t.wait(adj_b_loaded, 16)
                for b in range(G):
                    mm = pe.matmul(ps[:, 4 + b, QKVW:QKVW + E], adj_b[:, b, :], qk[:, b, E:QK],
                                   start=True, stop=True)
                mm.then_inc(ak_mm, 1)

            def c_wt(t):
                t.wait(wsum_ready, 1)
                pe.matmul(ps[0:G, 4, D:D + P], wsum[:], ident[:], start=True, stop=True).then_inc(wt_mm, 1)

            def c_wcol(t):
                t.wait(wnorm_ready, 1)
                pe.matmul(ps[:, 5, D:D + G], wnorm[:], ident[0:G, 0:G], start=True, stop=True)\
                  .then_inc(wcol_mm, 1)

            def c_x3t(t):
                turn_rows(t, x3, 2, 4, x3t_mm)

            def c_s1(t):
                for c in range(C):
                    t.wait(x3_hi_ready, 2, c + 1)
                    t.wait(x3_lo_ready, 2, c + 1)
                    for b in range(G):
                        mm = product(half(6 + b // 2, b % 2), split(x3_hi, x3_lo, c, b), weights(W_S1, D, c),
                                     c == 0 and b % 2 == 0, c == C - 1)
                        if c == C - 1 and b % 2:
                            mm.then_inc(s1_mm, 1)

            def gcn_turn(t, s, s_ready, done):
                for p in range(PAIRS):
                    t.wait(s_ready, 2, p + 1)
                    for c in range(C):
                        for b in (2 * p, 2 * p + 1):
                            mm = pe.matmul(quarter(4 + c, b), s[:, b, c * P:(c + 1) * P], adj_b[:, b, :],
                                           start=True, stop=True)
                        if p == PAIRS - 1:
                            mm.then_inc(done, 1)

            def c_s2(t):
                for c in range(C):
                    t.wait(h1_ready, 2, c + 1)
                    for b in range(G):
                        mm = pe.matmul(half(6 + b // 2, b % 2), h1_t[:, c, b, :], w_23[:, 0, c, :],
                                       start=(c == 0 and b % 2 == 0), stop=(c == C - 1), skip_group_check=True)
                        if c == C - 1 and b % 2:
                            mm.then_inc(s2_mm, 1)

            def c_s3(t, b):
                t.wait(h2_ready, 2)
                for c in range(C):
                    mm = pe.matmul(half(6 + b // 2, b % 2), h2_t[:, c, b, :], w_23[:, 1, c, :],
                                   start=(c == 0), stop=(c == C - 1))
                if b % 2:
                    mm.then_inc(s3_mm, 1)

            def c_out(t, p):
                t.wait(s3_ready, 2, p + 1)
                for b in (2 * p, 2 * p + 1):
                    mm = pe.matmul(half(6 + p, b % 2), adj_b[:, b, :], s3[:, b, :], start=True, stop=True)
                mm.then_inc(o_mm, 1)

            pe.wait_ge(w_loaded, W_LOADS)
            for m in range(C):
                for c in range(C):
                    mm = pe.matmul(ps[:, 0, 2 * m:2 * m + 2], wv_t[:, c, m * P:(m + 1) * P], aw_c[:, :, c],
                                   start=(c == 0), stop=(c == C - 1))
            for c in range(C):
                mm = pe.matmul(ps[:, 1, 0:2], bv_c[:, c:c + 1].broadcast_to([P, P]), aw_c[:, :, c],
                               start=(c == 0), stop=(c == C - 1))
            mm.then_inc(wva_mm, 1)
            pe.wait_ge(w_hi_ready, 2)
            pe.wait_ge(w_lo_ready, 2)
            pe.wait_ge(consts, CONSTS)
            pe.wait_ge(ident_ready, 1)
            pe.wait_ge(row_moved, 16)
            pe.wait_ge(c_loaded, 16 * H)

            def body(g, a=True, b=True, c=True):
                a, b, c = (Turn(pe, g - n) if on else None for n, on in enumerate((a, b, c)))
                if a:
                    a_y2(a, 0)
                    a_y2(a, 1)
                if c:
                    c_ak(c)
                if a:
                    a_si(a)
                    a_xw1(a, 0)
                if c:
                    c_wt(c)
                if a:
                    a_xw1(a, 1)
                    a_xw1(a, 2)
                    a_xw1(a, 3)
                if c:
                    c_wcol(c)
                if a:
                    a_rsum(a)
                    a_xw0(a, 0)
                    a_rt(a)
                    a_xw0(a, 1)
                    a_ty2(a)
                    a_xw0(a, 2)
                    a_xw0(a, 3)
                if c:
                    c_x3t(c)
                if a:
                    a_tz(a)
                if c:
                    c_s1(c)
                    gcn_turn(c, s1, s1_ready, h1_mm)
                if a:
                    a_x1t(a)
                if c:
                    c_s2(c)
                if a:
                    a_xpt(a)
                if c:
                    gcn_turn(c, s2, s2_ready, h2_mm)
                if a:
                    a_xp(a)
                    a_xct(a)
                if b:
                    b_x2t(b, c)
                for n in range(4):
                    if a:
                        a_scores(a, n // 2, n % 2)
                    if c:
                        c_s3(c, n)
                if a:
                    a_xh(a, 0)
                if c:
                    c_out(c, 0)
                if a:
                    a_xh(a, 1)
                if c:
                    c_out(c, 1)
                if a:
                    a_xh(a, 2)
                if b:
                    b_qkv(b, 0, c)
                    b_qkv(b, 1, c)
                if a:
                    a_xh(a, 3)
                if b:
                    b_qkv(b, 2, c)
                    b_qkv(b, 3, c)

            body(0, b=False, c=False)
            body(1, c=False)
            body(2)
            with pe.Fori(3, GROUPS) as g:
                body(g)
            body(GROUPS, a=False)
            body(GROUPS + 1, a=False, b=False)

        @block.scalar
        def _(act):
            copy, exp, ident_f = ACT.Copy, ACT.Exp, ACT.Identity
            act.wait_ge(seed_ready, 1)
            act.activation(act_seed[:], act_seed[:], exp).then_inc(w_hi_ready, 1)
            act.wait_ge(w_loaded, W_LOADS)
            act.wait_ge(wva_sb, 1)
            act.activation(w_hi[:], w_raw[:], copy).then_inc(w_hi_ready, 1)
            act.wait_ge(row_sum, 2)
            act.activation(row[0:1], row_raw[:], copy).then_inc(row_hi_ready, 1)

            def hi_part(dst, src_bank, mm, ready, t):
                for c in range(C):
                    t.wait(mm, 2, c + 1)
                    act.activation(dst[:, c], bank(src_bank + c), copy).then_inc(ready, 1)

            def out_of_psum(dst, src_bank, mm, ready, t):
                for p in range(PAIRS):
                    t.wait(mm, 2, p + 1)
                    act.activation(dst[:, 2 * p:2 * p + 2, :], bank(src_bank + p), copy).then_inc(ready, 1)

            def relu_of(dst, bias, mm, ready, t):
                for c in range(C):
                    t.wait(mm, 2, c + 1)
                    act.activation(dst[:, c], bank(4 + c), ACT.Relu, bias=bias[:, c:c + 1]).then_inc(ready, 1)

            def tanh(t, p, k):
                q = slice(2 * k, 2 * k + 2)
                t.wait(score_ready, 4, 2 * p + k + 1)
                act.activation(attn[:, p, q], attn[:, p, q], ACT.Tanh).then_inc(attn_ready, 1)

            def psum_pair(dst, src_bank, mm, ready, t, p):
                t.wait(mm, 2, p + 1)
                act.activation(dst[:, 2 * p:2 * p + 2, :], bank(src_bank + p), copy).then_inc(ready, 1)

            def body(g, a=True, b=True, c=True):
                a, b, c = (Turn(act, g - n) if on else None for n, on in enumerate((a, b, c)))
                if a:
                    for p in range(PAIRS):
                        a.wait(y2_mm, 2, p + 1)
                        act.activation(y2[:, 2 * p:2 * p + 2, :], ps[:, 2 * p:2 * p + 2, 0:Y2W], copy)\
                           .then_inc(y2_ready, 1)
                if c:
                    c.wait(wbias_ready, 1)
                    act.activation(wexp[:], ps[0:G, 4, D:D + P], exp, bias=wbias[:], scale=E ** -0.5,
                                   accum_out=wden[:]).then_inc(wexp_ready, 1)
                if a:
                    a.wait(zrelu_ready, 1)
                    act.activation(zexp[:], zrelu[:], exp).then_inc(zexp_ready, 1)
                    out_of_psum(zed, 2, zed_mm, zed_ready, a)
                if c:
                    hi_part(x3_hi, 4, x3t_mm, x3_hi_ready, c)
                    out_of_psum(s1, 6, s1_mm, s1_ready, c)
                    relu_of(h1_t, b1_c, h1_mm, h1_ready, c)
                if a:
                    hi_part(x1_hi, 2, x1t_mm, x1_hi_ready, a)
                if c:
                    out_of_psum(s2, 6, s2_mm, s2_ready, c)
                if a:
                    for m in range(C):
                        a.wait(xpt_mm, 2, m + 1)
                        act.activation(xp_t[:, m], bank(m), ident_f, bias=bp_c[:, m:m + 1])\
                           .then_inc(xpt_ready, 1)
                if c:
                    relu_of(h2_t, b2_c, h2_mm, h2_ready, c)
                if a:
                    for m in range(C):
                        a.wait(xct_mm, 2, m + 1)
                        act.activation(xc_t[:, m], bank(m), copy).then_inc(xct_ready, 1)
                if b:
                    hi_part(x2_hi, 4, x2t_mm, x2_hi_ready, b)
                    b.wait(y_ready[2], 2, 0)
                    act.activation(x2_kept[:], x2[:], copy).then_inc(x2_kept_ready, 1)
                if a:
                    tanh(a, 0, 0)
                    tanh(a, 0, 1)
                if c:
                    psum_pair(s3, 6, s3_mm, s3_ready, c, 0)
                if a:
                    tanh(a, 1, 0)
                if c:
                    psum_pair(s3, 6, s3_mm, s3_ready, c, 1)
                if a:
                    tanh(a, 1, 1)
                if b:
                    b.wait(qkv_mm, 4)
                    act.activation(qk[:], ps[:, 4:8, D:QKVW], copy).then_inc(qk_ready, 1)

            body(0, b=False, c=False)
            body(1, c=False)
            body(2)
            with act.Fori(3, GROUPS) as g:
                body(g)
            body(GROUPS, a=False)
            body(GROUPS + 1, a=False, b=False)

        @block.vector
        def _(dve):
            dve.wait_ge(wva_mm, 1)
            for m in range(C):
                a = W_Y2 + m * Y2W + D
                cp = dve.tensor_copy(w_raw[:, a:a + 2], ps[:, 0, 2 * m:2 * m + 2])
            cp.then_inc(wva_sb, 1)
            dve.tensor_copy(z_bias[:], ps[:, 1, 0:2]).then_inc(zb_sb, 1)
            dve.tensor_tensor(row_raw[:], bk_row[:, 0, :], bk_row[:, 1, :], ALU.add).then_inc(row_sum, 1)
            dve.wait_ge(zb_sb, 1)
            dve.scalar_tensor_tensor(z_const[:], z_bias[:, 0:1], ab_c[:, 0:1], z_bias[:, 1:2],
                                     ALU.add, ALU.add).then_inc(z_const_ready, 1)
            dve.wait_ge(row_sum, 1)
            dve.tensor_tensor(row_raw[:], row_raw[:], bk_row[:, 2, :], ALU.add).then_inc(row_sum, 1)
            dve.wait_ge(w_hi_ready, 2)
            dve.tensor_tensor(w_lo[:], w_raw[:], w_hi[:].bitcast(F32), ALU.subtract).then_inc(w_lo_ready, 2)
            dve.wait_ge(row_hi_ready, 1)
            dve.tensor_tensor(row_lo[:], row_raw[:], row[0:1].bitcast(F32), ALU.subtract)\
               .then_inc(row_lo_ready, 1)
            dve.wait_ge(z_const_ready, 1)

            def lo_part(dst, hi, src_bank, hi_ready, ready, t):
                for c in range(C):
                    t.wait(hi_ready, 2, c + 1)
                    dve.tensor_tensor(dst[:, c], bank(src_bank + c), hi[:, c].bitcast(F32), ALU.subtract)\
                       .then_inc(ready, 1)

            def norm_stats(n, y, t):
                t.wait(y_ready[n], 2)
                for b in range(G):
                    op = dve.bn_stats(st[n][:, b, :], y[:, b, :])
                op.then_inc(st_ready[n], 1)
                t.wait(st_ready[n], 1)
                dve.memset(anchor[:, n:n + 1], 0.0)
                for b in range(G):
                    op = dve.bn_aggr(mv[n][:, b, :], st[n][:, b, :])
                op.then_inc(mv_ready[n], 1)
                t.wait(mv_ready[n], 1)
                dve.tensor_scalar(ve[n][:], mv[n][:, :, 1], EPS, None, ALU.add).then_inc(ve_ready[n], 1)

            def norm_rows(n, y, dst, t):
                t.wait(rs_ready[n], 1)
                for b in range(G):
                    op = dve.tensor_scalar(dst[:, b, :], y[:, b, :], mv[n][:, b, 0:1], rs[n][:, b:b + 1],
                                           ALU.subtract, ALU.mult)
                    if b % 2:
                        op.then_inc(x_ready[n], 1)

            def sum_relu(n, dst, mm, x_in, t, p):
                t.wait(mm, 2, p + 1)
                pair = slice(2 * p, 2 * p + 2)
                dve.scalar_tensor_tensor(dst[:, pair, :], bank(p), 0.0, x_in[:, pair, :],
                                         ALU.max, ALU.add).then_inc(y_ready[n], 1)

            def scores(t, p, k):
                t.wait(score_mm, 4, 2 * p + k + 1)
                pair = adj_a[:, 2 * p:2 * p + 2, :].rearrange("p b n -> p (b n)")
                dve.tensor_tensor(
                    attn[:, p, 2 * k:2 * k + 2].rearrange("p q c b n -> p (q c) (b n)"),
                    ps[:, 2 * k:2 * k + 2, :].rearrange("p q (c m) -> p (q c) m", c=C),
                    pair.unsqueeze(1).broadcast_to([P, 2 * C, 2 * P]), ALU.mult).then_inc(score_ready, 1)

            def weigh(t, p):
                for b in (2 * p, 2 * p + 1):
                    op = dve.scalar_tensor_tensor(yb[:, b, :], ps[:, 4 + b, 0:D], wcol[:, b:b + 1],
                                                  x2_kept[:, b, :], ALU.mult, ALU.add)
                op.then_inc(y_ready[2], 1)

            def body(g, a=True, b=True, c=True):
                a, b, c = (Turn(dve, g - n) if on else None for n, on in enumerate((a, b, c)))
                if c:
                    c.wait(ak_mm, 1)
                    dve.tensor_tensor(qak[:], qk[:, :, 0:E], ps[:, 4:8, QKVW:QKVW + E], ALU.mult)\
                       .then_inc(qak_ready, 1)
                    c.wait(qak_ready, 1)
                    dve.reduce_sum(wsum[:], qak[:], AX_X).then_inc(wsum_ready, 1)
                if a:
                    a.wait(si_mm, 1)
                    dve.scalar_tensor_tensor(zsum[:], bank(0).rearrange("p (b n) -> p b n", b=G), z_const[:, 0:1],
                                             y2[:, :, D:D + 1].broadcast_to([P, G, P]),
                                             ALU.add, ALU.add).then_inc(zsum_ready, 1)
                    a.wait(zsum_ready, 1)
                    dve.scalar_tensor_tensor(zrelu[:], zsum[:], SLOPE, zsum[:], ALU.mult, ALU.max)\
                       .then_inc(zrelu_ready, 1)
                if c:
                    c.wait(wt_mm, 1)
                    dve.reduce_max(wmax[:], ps[0:G, 4, D:D + P], AX_X).then_inc(wmax_ready, 1)
                    c.wait(wmax_ready, 1)
                    dve.tensor_scalar(wbias[:], wmax[:], -E ** -0.5, None, ALU.mult).then_inc(wbias_ready, 1)
                    c.wait(wexp_ready, 1)
                    dve.reciprocal(wrec[:], wden[:]).then_inc(wrec_ready, 1)
                    c.wait(wrec_ready, 1)
                    dve.tensor_scalar(wnorm[:], wexp[:], wrec[:, 0:1], None, ALU.mult).then_inc(wnorm_ready, 1)
                    c.wait(wcol_mm, 1)
                    dve.tensor_copy(wcol[:], ps[:, 5, D:D + G]).then_inc(wcol_ready, 1)
                if a:
                    a.wait(rsum_mm, 1)
                    dve.tensor_scalar(rsum[:], ps[:, 1, 0:G], TINY, None, ALU.add).then_inc(rsum_ready, 1)
                    a.wait(rsum_ready, 1)
                    dve.reciprocal(rrec[:], rsum[:]).then_inc(rrec_ready, 1)
                if c:
                    c.wait(x2_kept_ready, 1)
                    c.wait(wcol_ready, 1)
                    weigh(c, 0)
                if a:
                    a.wait(rt_mm, 1)
                    dve.tensor_tensor(trans[:], alpha[:], bank(1).rearrange("p (b n) -> p b n", b=G), ALU.mult).then_inc(trans_ready, 1)
                if c:
                    weigh(c, 1)
                    norm_stats(2, yb, c)
                if c:
                    norm_rows(2, yb, x3, c)
                    lo_part(x3_lo, x3_hi, 4, x3_hi_ready, x3_lo_ready, c)
                if a:
                    a.wait(x_loaded, 16)
                    sum_relu(0, ya, h_mm, xa, a, 0)
                    sum_relu(0, ya, h_mm, xa, a, 1)
                    norm_stats(0, ya, a)
                    norm_rows(0, ya, x1, a)
                    lo_part(x1_lo, x1_hi, 2, x1_hi_ready, x1_lo_ready, a)
                    for p in range(PAIRS):
                        a.wait(xp_mm, 2, p + 1)
                        dve.tensor_copy(xp[:, 2 * p:2 * p + 2, :], bank(2 + p)).then_inc(xp_ready, 1)
                if b:
                    lo_part(x2_lo, x2_hi, 4, x2_hi_ready, x2_lo_ready, b)
                if a:
                    for n in range(4):
                        scores(a, n // 2, n % 2)
                if c:
                    c.wait(x3b_ready, 1)
                    for p in range(PAIRS):
                        c.wait(o_mm, 2, p + 1)
                        pair = slice(2 * p, 2 * p + 2)
                        dve.tensor_tensor(yo[:, pair, :], bank(6 + p), x3b[:, pair, :], ALU.add)\
                           .then_inc(y_ready[3], 1)
                    norm_stats(3, yo, c)
                if a:
                    sum_relu(1, ya, xh_mm, x1, a, 0)
                    sum_relu(1, ya, xh_mm, x1, a, 1)
                    norm_stats(1, ya, a)
                if c:
                    c.wait(stored, 16, 0)
                    norm_rows(3, yo, x4, c)
                if a:
                    if b:
                        b.wait(x2_kept_ready, 1)
                    norm_rows(1, ya, x2, a)

            body(0, b=False, c=False)
            body(1, c=False)
            body(2)
            with dve.Fori(3, GROUPS) as g:
                body(g)
            body(GROUPS, a=False)
            body(GROUPS + 1, a=False, b=False)

        @block.gpsimd
        def _(pool):
            pool.memset(c_t[:], 0.0).then_inc(c_zeroed, 1)
            pool.memset(act_seed[:], 0.0).then_inc(seed_ready, 1)
            pool.memset(ident[:], 0.0).then_inc(consts, 1)
            pool.memset(ones[:], 1.0).then_inc(consts, 1)
            pool.memset(neg_half[:], -0.5).then_inc(consts, 1)
            pool.wait_ge(consts, 3)
            pool.affine_select(out=ident[:], in_=ident[:], compare_op=ALU.not_equal, fill=1.0, base=0,
                               pattern=[[-1, P]], channel_multiplier=1).then_inc(ident_ready, 1)
            pool.tensor_copy(ones_r[:], ones[0:2, :]).then_inc(consts, 2)

            def split_x(g):
                t = Turn(pool, g)
                t.wait(xw0_mm, 1, 0)
                t.wait(xt_loaded, 16)
                one = ones[:, 0:1].unsqueeze(1).unsqueeze(1).broadcast_to([P, C, G, P])
                pool.tensor_tensor(xa_hi[:], xa_t[:], one, ALU.mult).then_inc(xa_hi_ready, 1)
                t.wait(xa_hi_ready, 1)
                pool.tensor_tensor(xa_lo[:], xa_t[:], xa_hi[:].bitcast(F32), ALU.subtract)\
                    .then_inc(xa_lo_ready, 1)

            def a_alpha(t):
                t.wait(adj_a_loaded, 16)
                t.wait(zexp_ready, 1)
                pool.tensor_tensor(alpha[:], adj_a[:], zexp[:], ALU.mult).then_inc(alpha_ready, 1)

            def c_bias(t):
                t.wait(x_ready[2], 2)
                b3_all = b3_rows[:].unsqueeze(1).broadcast_to([P, G, D])
                pool.tensor_tensor(x3b[:], x3[:], b3_all, ALU.add).then_inc(x3b_ready, 1)

            def norm_scale(n, t):
                t.wait(ve_ready[n], 1)
                pool.tensor_tensor(rs[n][:], ve[n][:], neg_half[:], ALU.pow).then_inc(rs_ready[n], 1)

            def body(g, a=True, c=True, more=True):
                a, c = Turn(pool, g) if a else None, Turn(pool, g - 2) if c else None
                if a:
                    a_alpha(a)
                if c:
                    norm_scale(2, c)
                if a:
                    norm_scale(0, a)
                if c:
                    c_bias(c)
                if more:
                    split_x(g + 1)
                if c:
                    norm_scale(3, c)
                if a:
                    norm_scale(1, a)

            pool.wait_ge(w_loaded, W_LOADS)
            split_x(0)
            body(0, c=False)
            body(1, c=False)
            body(2)
            with pool.Fori(3, GROUPS - 1) as g:
                body(g)
            body(GROUPS - 1, more=False)
            body(GROUPS, a=False, more=False)
            body(GROUPS + 1, a=False, more=False)


_OUT = (B, P, D)


def kernel(x, adj, L0_gnn_Wv, L0_gnn_bv, L0_gnn_aw, L0_gnn_ab, L0_gnn_Wk, L0_gnn_bk, L1_gnn_Wp, L1_gnn_bp,
           L1_gnn_C, L2_gnn_W_qk, L2_gnn_W_v, L3_gnn_W1, L3_gnn_b1, L3_gnn_W2, L3_gnn_b2, L3_gnn_W3, L3_gnn_b3):
    import numpy as np
    import concourse.bacc as bacc
    from concourse.bass_utils import run_bass_kernel_spmd

    def lay(a, shape, order):
        return np.ascontiguousarray(np.asarray(a).reshape(shape).transpose(order))

    def chunks(w):
        w = np.asarray(w)
        return lay(w, (C, P, w.shape[1]), (1, 0, 2))

    wk, qk = np.asarray(L0_gnn_Wk), np.asarray(L2_gnn_W_qk)
    wp = lay(L1_gnn_Wp, (H, D, DH), (1, 0, 2)).reshape(D, D)
    qkv = np.concatenate([np.asarray(L2_gnn_W_v), qk]).T
    wraw = np.concatenate([chunks(w).reshape(P, -1) for w in (wk[2], wk[1], wk[0], wp, qkv, L3_gnn_W1)], axis=1)
    arrays = {
        "x": np.ascontiguousarray(np.asarray(x)),
        "xT": lay(x, (GROUPS, G, P, C, P), (0, 4, 3, 1, 2)),
        "aT": lay(adj, (GROUPS, G, P, P), (0, 3, 1, 2)),
        "wraw": np.ascontiguousarray(wraw),
        "wvT": chunks(np.asarray(L0_gnn_Wv).T),
        "awc": lay(L0_gnn_aw, (2, C, P), (2, 0, 1)),
        "bvc": lay(L0_gnn_bv, (C, P), (1, 0)),
        "ab": np.ascontiguousarray(np.broadcast_to(np.asarray(L0_gnn_ab).reshape(1, 1), (P, 1))),
        "bk": lay(L0_gnn_bk, (1, 3, D), (0, 1, 2)),
        "bpc": lay(L1_gnn_bp, (C, P), (1, 0)),
        "cT": lay(L1_gnn_C, (H, DH, DH), (0, 2, 1)),
        "b1c": lay(L3_gnn_b1, (C, P), (1, 0)),
        "b2c": lay(L3_gnn_b2, (C, P), (1, 0)),
        "w23": np.ascontiguousarray(np.stack([chunks(L3_gnn_W2), chunks(L3_gnn_W3)], axis=1)),
        "b3": np.ascontiguousarray(np.broadcast_to(np.asarray(L3_gnn_b3).reshape(1, D), (P, D))),
    }
    nc = bacc.Bacc("TRN2", target_bir_lowering=False, num_devices=1)
    args = [nc.dram_tensor(f"in_{n}", a.shape, mybir.dt.from_np(a.dtype), kind="ExternalInput").ap()
            for n, a in arrays.items()]
    args.append(nc.dram_tensor("out", _OUT, F32, kind="ExternalOutput").ap())
    build(nc, *args)
    r = run_bass_kernel_spmd(nc, [{f"in_{n}": a for n, a in arrays.items()}], core_ids=[0])
    return r.results[0]["out"]
```

```python
from contextlib import ExitStack

import concourse.bass as bass
from concourse import mybir

F32 = mybir.dt.float32
F32R = mybir.dt.float32r
ALU = mybir.AluOpType
ACT = mybir.ActivationFunctionType
AX_X = mybir.AxisListType.X

P = 128
B = 64
D = 256
C = D // P
G = 4
GROUPS = B // G
PAIRS = G // 2
H = 8
DH = D // H
QH = P // DH
E = 64
QK = 2 * E
EPS = 1e-5
TINY = 1e-12
SLOPE = 0.2

W_Y2, Y2W = 0, D + 2
W_Z = W_Y2 + C * Y2W
W_H = W_Z + C * D
W_P = W_H + C * D
W_QKV, QKVW = W_P + C * D, D + QK
W_S1 = W_QKV + C * QKVW
W_S2 = W_S1 + C * D
W_S3 = W_S2 + C * D
W_END = W_S3 + C * D


class Lane:

    def __init__(self, ps, spare, turned=False):
        self.ps, self.spare, self.turned = ps, spare, turned

    def norms(self, sb, name, which):
        self.st = {n: sb(f"st{n}_{name}", [P, G, 6]) for n in which}
        self.mv = {n: sb(f"mv{n}_{name}", [P, G, 2]) for n in which}
        self.ve = {n: sb(f"ve{n}_{name}", [P, G]) for n in which}
        self.rs = {n: sb(f"rs{n}_{name}", [P, G]) for n in which}
        self.anchor = {n: sb(f"anchor{n}_{name}", [1, 1]) for n in which}

    def at(self, n):
        return (n + 2) % 4 if self.turned else n

    def bank(self, n):
        return self.ps[:, self.at(n), :]

    def two(self, n):
        return self.ps[:, self.at(n):self.at(n) + 2, :]

    def half(self, n, j):
        return self.bank(n)[:, j * D:(j + 1) * D]

    def quarter(self, n, b):
        return self.bank(n)[:, b * P:(b + 1) * P]


class Carve:

    def __init__(self, space, skip=0):
        self.space, self.at = space, skip

    def take(self, *shape):
        size = 1
        for n in shape:
            size *= n
        flat = self.space[:, self.at:self.at + size]
        self.at += size
        axes = [f"a{i}" for i in range(len(shape))]
        return flat.rearrange(f"p ({' '.join(axes)}) -> p {' '.join(axes)}", **dict(zip(axes, shape)))


class Turn:

    def __init__(self, engine, group, lane, first=False):
        self.engine, self.group, self.m, self.known = engine, group, lane, {}
        self.first = first or lane.spare or isinstance(group, int) and group == 0

    def at(self, each, k=None):
        k = each if k is None else k
        if isinstance(self.group, int):
            return self.group * each + k
        if (each, k) not in self.known:
            self.known[each, k] = self.engine.snap(self.group * each + k)
        return self.known[each, k]


def build(nc, x, xT, aT, wraw, wvT, awc, bvc, ab, bk, bpc, cT, b1c, b2c, b3, out):
    with ExitStack() as ctx:
        def sb(name, shape, dt=F32):
            return ctx.enter_context(nc.sbuf_tensor(name, shape, dt))

        def sem(name):
            return ctx.enter_context(nc.semaphore(name))

        w_raw = sb("w_raw", [P, W_END])
        w_hi = sb("w_hi", [P, W_END], F32R)
        w_lo = sb("w_lo", [P, W_END], F32R)
        aw_c = sb("aw_c", [P, 2, C])
        bv_c = sb("bv_c", [P, C])
        ab_c = sb("ab_c", [P, 1])
        z_bias = sb("z_bias", [P, 2])
        z_const = sb("z_const", [P, 1])
        bk_row = sb("bk_row", [1, 3, D])
        row_raw = sb("row_raw", [1, D])
        row = sb("row", [2, D], F32R)
        row_lo = sb("row_lo", [1, D], F32R)
        b3_rows = sb("b3_rows", [P, D])
        bp_c = sb("bp_c", [P, C])
        b1_c = sb("b1_c", [P, C])
        b2_c = sb("b2_c", [P, C])
        c_t = sb("c_t", [P, C, P])
        ident = sb("ident", [P, P])
        ones = sb("ones", [P, P])
        ones_r = sb("ones_r", [2, P], F32R)
        neg_half = sb("neg_half", [P, G])
        act_seed = sb("act_seed", [P, 1])
        x2 = sb("x2", [P, G, D])

        ps = ctx.enter_context(nc.psum_tensor("ps", [P, 8, 512], F32))
        SPACE_A = 14 * G * D + G * Y2W + 6 * G * P
        SPACE_C = 8 * G * D + G * Y2W
        space_a = sb("space_a", [P, SPACE_A])
        space_c = sb("space_c", [P, SPACE_C])
        split_a = sb("split_a", [P, 4 * C * G * P], F32R)
        split_c = sb("split_c", [P, 4 * C * G * P], F32R)

        wv_t = Carve(space_c, SPACE_C - C * D).take(C, D)

        def lane_a(name, banks, carve, split, late, spare):
            take = carve.take
            lane = Lane(ps[:, banks:banks + 4], spare, turned=spare)
            lane.adj = take(G, P)
            lane.xa = take(G, D)
            lane.xa_t = take(C, G, P)
            lane.xa_hi = split.take(C, G, P)
            lane.xa_lo = split.take(C, G, P)
            lane.y2 = take(G, Y2W)
            lane.zsum = take(G, P)
            lane.zrelu = take(G, P)
            lane.trans = late.take(G, P)
            lane.zed = late.take(G, D)
            lane.x1 = late.take(G, D)
            lane.attn = take(PAIRS, QH, C, 2, P)
            lane.ya = late.take(G, D)
            lane.rsum = sb(f"rsum_{name}", [P, G])
            lane.rrec = sb(f"rrec_{name}", [P, G])
            lane.norms(sb, name, (0, 1))
            if spare:
                lane.zexp, lane.alpha, lane.xp, lane.xc_t = lane.zsum, lane.zrelu, lane.zed, lane.xa_t
                lane.x1_hi, lane.x1_lo = lane.xa_hi, lane.xa_lo
                lane.xp_t = lane.y2.rearrange("p b w -> p (b w)")[:, 0:C * G * P]\
                                .rearrange("p (c b n) -> p c b n", c=C, b=G)
            else:
                lane.zexp, lane.alpha, lane.xp, lane.xc_t = take(G, P), take(G, P), take(G, D), take(C, G, P)
                lane.x1_hi, lane.x1_lo = split.take(C, G, P), split.take(C, G, P)
                lane.xp_t = take(C, G, P)
            return lane

        def lane_bc(name, banks, carve, split, late, spare, adj):
            take = carve.take
            lane = Lane(ps[:, banks:banks + 4], spare)
            lane.adj = adj
            lane.x2_kept = take(G, D)
            lane.x2_hi = split.take(C, G, P)
            lane.x2_lo = split.take(C, G, P)
            lane.qk = take(G, QK)
            lane.qak = take(G, E)
            lane.x3_hi = split.take(C, G, P)
            lane.x3_lo = split.take(C, G, P)
            lane.yb = take(G, D)
            lane.x3 = take(G, D)
            lane.x3b = take(G, D)
            lane.s = take(G, D)
            lane.h_t = take(C, G, P)
            lane.h_hi, lane.h_lo = lane.x3_hi, lane.x3_lo
            lane.x4 = late.take(G, D)
            lane.yo = late.take(G, D)
            lane.wsum = sb(f"wsum_{name}", [P, G])
            lane.wmax = sb(f"wmax_{name}", [G, 1])
            lane.wbias = sb(f"wbias_{name}", [G, 1])
            lane.wexp = take(P)[0:G]
            lane.wden = sb(f"wden_{name}", [G, 1])
            lane.wrec = sb(f"wrec_{name}", [G, 1])
            lane.wnorm = take(P)[0:G]
            lane.wcol = sb(f"wcol_{name}", [P, G])
            lane.norms(sb, name, (2, 3))
            return lane

        a_carve = Carve(space_a)
        A_LANE = lane_a("a", 0, a_carve, Carve(split_a), a_carve, False)
        C_LANE = lane_bc("c", 4, Carve(space_c, G * P), Carve(split_c), Carve(w_raw), False,
                         space_c[:, 0:G * P].rearrange("p (b n) -> p b n", b=G))
        A_SPARE = lane_a("a_spare", 4, Carve(space_c, G * P), Carve(split_c), Carve(w_raw), True)
        a_carve = Carve(space_a, G * P)
        C_SPARE = lane_bc("c_spare", 0, a_carve, Carve(split_a), a_carve, True, A_LANE.adj)

        wva_loaded = sem("wva_loaded")
        bias_loaded = sem("bias_loaded")
        w_loaded = [sem(f"w{n}_loaded") for n in range(8)]
        w_hi_ready = sem("w_hi_ready")
        w_lo_ready = sem("w_lo_ready")
        rest_loaded = sem("rest_loaded")
        c_zeroed = sem("c_zeroed")
        c_loaded = sem("c_loaded")
        consts = sem("consts")
        ident_ready = sem("ident_ready")
        seed_ready = sem("seed_ready")
        wva_mm = sem("wva_mm")
        wva_sb = sem("wva_sb")
        zb_sb = sem("zb_sb")
        z_const_ready = sem("z_const_ready")
        row_sum = sem("row_sum")
        row_hi_ready = sem("row_hi_ready")
        row_lo_ready = sem("row_lo_ready")
        row_moved = sem("row_moved")
        x_loaded = sem("x_loaded")
        xt_loaded = sem("xt_loaded")
        adj_a_loaded = sem("adj_a_loaded")
        adj_c_loaded = sem("adj_c_loaded")
        stored = sem("stored")
        xa_hi_ready = sem("xa_hi_ready")
        xa_lo_ready = sem("xa_lo_ready")
        y2_mm = sem("y2_mm")
        y2_ready = sem("y2_ready")
        si_mm = sem("si_mm")
        zsum_ready = sem("zsum_ready")
        zrelu_ready = sem("zrelu_ready")
        zexp_ready = sem("zexp_ready")
        alpha_ready = sem("alpha_ready")
        rsum_mm = sem("rsum_mm")
        rsum_ready = sem("rsum_ready")
        rrec_ready = sem("rrec_ready")
        rt_mm = sem("rt_mm")
        trans_ready = sem("trans_ready")
        xw0_mm = sem("xw0_mm")
        zed_mm = sem("zed_mm")
        zed_ready = sem("zed_ready")
        h_mm = sem("h_mm")
        x1t_mm = sem("x1t_mm")
        x1_hi_ready = sem("x1_hi_ready")
        x1_lo_ready = sem("x1_lo_ready")
        xpt_mm = sem("xpt_mm")
        xpt_ready = sem("xpt_ready")
        xp_mm = sem("xp_mm")
        xp_ready = sem("xp_ready")
        xct_mm = sem("xct_mm")
        xct_ready = sem("xct_ready")
        score_mm = sem("score_mm")
        score_ready = sem("score_ready")
        attn_ready = sem("attn_ready")
        xh_mm = sem("xh_mm")
        x2t_mm = sem("x2t_mm")
        x2_hi_ready = sem("x2_hi_ready")
        x2_lo_ready = sem("x2_lo_ready")
        x2_kept_ready = sem("x2_kept_ready")
        qkv_mm = sem("qkv_mm")
        qk_ready = sem("qk_ready")
        ak_mm = sem("ak_mm")
        qak_ready = sem("qak_ready")
        wsum_ready = sem("wsum_ready")
        wt_mm = sem("wt_mm")
        wmax_ready = sem("wmax_ready")
        wbias_ready = sem("wbias_ready")
        wexp_ready = sem("wexp_ready")
        wrec_ready = sem("wrec_ready")
        wnorm_ready = sem("wnorm_ready")
        wcol_mm = sem("wcol_mm")
        wcol_ready = sem("wcol_ready")
        x3b_ready = sem("x3b_ready")
        x3t_mm = sem("x3t_mm")
        x3_hi_ready = sem("x3_hi_ready")
        x3_lo_ready = sem("x3_lo_ready")
        s1_mm = sem("s1_mm")
        s1_ready = sem("s1_ready")
        h1_mm = sem("h1_mm")
        h1_hi_ready = sem("h1_hi_ready")
        h1_ready = sem("h1_ready")
        h1_lo_ready = sem("h1_lo_ready")
        s2_mm = sem("s2_mm")
        s2_ready = sem("s2_ready")
        h2_mm = sem("h2_mm")
        h2_hi_ready = sem("h2_hi_ready")
        h2_ready = sem("h2_ready")
        h2_lo_ready = sem("h2_lo_ready")
        s3_mm = sem("s3_mm")
        s3_ready = sem("s3_ready")
        o_mm = sem("o_mm")
        y_ready = [sem(f"ln{n}_in_ready") for n in range(4)]
        st_ready = [sem(f"ln{n}_st_ready") for n in range(4)]
        mv_ready = [sem(f"ln{n}_mv_ready") for n in range(4)]
        ve_ready = [sem(f"ln{n}_ve_ready") for n in range(4)]
        rs_ready = [sem(f"ln{n}_rs_ready") for n in range(4)]
        x_ready = [sem(f"ln{n}_out_ready") for n in range(4)]

        edges = (W_Y2, W_Z, W_H, W_P, W_QKV, W_S1, W_S2, W_S3, W_END)
        sections = list(zip(edges, edges[1:]))
        wva_loads = [(aw_c[:], awc), (wv_t[:], wvT), (bv_c[:], bvc)]
        bias_loads = [(ab_c[:], ab), (bk_row[:], bk)]
        rest_loads = [(bp_c[:], bpc), (b1_c[:], b1c), (b2_c[:], b2c), (b3_rows[:], b3)]
        CONSTS = 5

        x_dram = x.rearrange("(i b) n d -> i n b d", b=G)
        out_dram = out.rearrange("(i b) n d -> i n b d", b=G)

        block = ctx.enter_context(nc.Block())

        @block.sync
        def _(sp):
            def load_xt(t):
                if not t.first:
                    sp.wait_ge(xa_lo_ready, t.at(1, 0))
                sp.dma_start(t.m.xa_t, xT[t.group]).then_inc(xt_loaded, 16)

            def load_x(t):
                if not t.first:
                    sp.wait_ge(y_ready[0], t.at(2, 0))
                sp.dma_start(t.m.xa, x_dram[t.group]).then_inc(x_loaded, 16)

            def load_adj_a(t):
                if not t.first:
                    sp.wait_ge(score_ready, t.at(4, 0))
                sp.dma_start(t.m.adj, aT[t.group]).then_inc(adj_a_loaded, 16)

            def load_adj_c(t):
                if not t.first:
                    sp.wait_ge(o_mm, t.at(2, 0))
                sp.dma_start(t.m.adj, aT[t.group]).then_inc(adj_c_loaded, 16)

            def store(t):
                sp.wait_ge(x_ready[3], t.at(2))
                sp.dma_start(out_dram[t.group], t.m.x4).then_inc(stored, 16)

            def load_weights(n):
                a, b = sections[n]
                if n == 0:
                    sp.dma_start(w_raw[:, a:b].rearrange("p (c w) -> p c w", c=C)[:, :, 0:D],
                                 wraw[:, 0:C * D].rearrange("p (c w) -> p c w", c=C)).then_inc(w_loaded[0], 16)
                else:
                    a -= C * 2
                    sp.dma_start(w_raw[:, sections[n][0]:b], wraw[:, a:b - C * 2]).then_inc(w_loaded[n], 16)

            def head():
                a0, a1 = Turn(sp, 0, A_LANE), Turn(sp, 1, A_SPARE)
                for dst, src in wva_loads:
                    sp.dma_start(dst, src).then_inc(wva_loaded, 16)
                load_xt(a0)
                load_weights(0)
                for dst, src in bias_loads:
                    sp.dma_start(dst, src).then_inc(bias_loaded, 16)
                load_adj_a(a0)
                load_weights(1)
                sp.wait_ge(xt_loaded, a0.at(16))
                load_xt(a1)
                load_weights(2)
                sp.wait_ge(row_lo_ready, 1)
                sp.dma_start(row[1:2].bitcast(F32), row_lo[:].bitcast(F32)).then_inc(row_moved, 16)
                load_x(a0)
                sp.wait_ge(adj_a_loaded, a0.at(16))
                load_adj_a(a1)
                load_weights(3)
                for dst, src in rest_loads:
                    sp.dma_start(dst, src).then_inc(rest_loaded, 16)
                sp.wait_ge(c_zeroed, 1)
                for h in range(H):
                    r = DH * (h % QH)
                    sp.dma_start(c_t[r:r + DH, h // QH, r:r + DH], cT[h]).then_inc(c_loaded, 16)
                sp.wait_ge(x_loaded, a0.at(16))
                load_x(a1)
                for n in range(4, len(sections)):
                    load_weights(n)
                sp.wait_ge(xt_loaded, a1.at(16))
                a2 = Turn(sp, 2, A_LANE)
                load_xt(a2)
                sp.wait_ge(x_loaded, a1.at(16))
                load_x(a2)
                load_adj_c(Turn(sp, 0, C_LANE))
                sp.wait_ge(adj_a_loaded, a1.at(16))
                load_adj_a(a2)

            def body(g, more=True):
                a, b, c = Turn(sp, g + 1, A_LANE), Turn(sp, g - 1, C_LANE), Turn(sp, g - 2, C_LANE)
                if more:
                    load_xt(a)
                    load_x(a)
                load_adj_c(b)
                store(c)
                if more:
                    load_adj_a(a)

            head()
            body(2)
            with sp.Fori(3, GROUPS - 1) as g:
                body(g)
            body(GROUPS - 1, more=False)
            store(Turn(sp, GROUPS - 2, C_LANE))
            last = Turn(sp, GROUPS - 1, C_SPARE)
            for p in range(PAIRS):
                pair = slice(2 * p, 2 * p + 2)
                sp.wait_ge(x_ready[3], last.at(2, p + 1))
                sp.dma_start(out_dram[last.group][:, pair, :], last.m.x4[:, pair, :]).then_inc(stored, 16)
            sp.wait_ge(stored, 16 * (GROUPS + 1))

        @block.tensor
        def _(pe):
            def product(dst, left, right, start, stop):
                pe.matmul(dst, left[1], right[0], start=start, stop=False, skip_group_check=True)
                pe.matmul(dst, left[0], right[1], start=False, stop=False, skip_group_check=True)
                return pe.matmul(dst, left[0], right[0], start=False, stop=stop, skip_group_check=True)

            def weights(at, width, c):
                a = at + c * width
                return w_hi[:, a:a + width], w_lo[:, a:a + width]

            def split(hi, lo, c, b):
                return hi[:, c, b, :], lo[:, c, b, :]

            def rows_times(dst, hi, lo, b, at, width, start, stop):
                for c in range(C):
                    mm = product(dst, split(hi, lo, c, b), weights(at, width, c),
                                 start and c == 0, stop and c == C - 1)
                return mm

            def turn_rows(t, src, n, first, done):
                for p in range(PAIRS):
                    pe.wait_ge(x_ready[n], t.at(2, p + 1))
                    for c in range(C):
                        for b in (2 * p, 2 * p + 1):
                            mm = pe.transpose(t.m.quarter(first + c, b), src[:, b, c * P:(c + 1) * P], ident[:])
                        if p == PAIRS - 1:
                            mm.then_inc(done, 1)

            def a_y2(t, p):
                pe.wait_ge(xa_hi_ready, t.at(1))
                pe.wait_ge(xa_lo_ready, t.at(1))
                if not t.first and p:
                    pe.wait_ge(score_ready, t.at(4, 0))
                if not t.first and not p:
                    pe.wait_ge(y_ready[1], t.at(2, 0))
                for b in (2 * p, 2 * p + 1):
                    mm = rows_times(t.m.bank(b)[:, 0:Y2W], t.m.xa_hi, t.m.xa_lo, b, W_Y2, Y2W, True, True)
                mm.then_inc(y2_mm, 1)

            def a_xw1(t, b):
                pe.wait_ge(y2_ready, t.at(2, 1))
                rows_times(t.m.half(2 + b // 2, b % 2), t.m.xa_hi, t.m.xa_lo, b, W_Z, D, b % 2 == 0, False)

            def a_si(t):
                pe.wait_ge(y2_ready, t.at(2))
                for b in range(G):
                    mm = pe.transpose(t.m.quarter(0, b), t.m.y2[:, b, D + 1:D + 2].broadcast_to([P, P]),
                                      ident[:])
                mm.then_inc(si_mm, 1)

            def a_rsum(t):
                pe.wait_ge(alpha_ready, t.at(1))
                for b in range(G):
                    mm = pe.matmul(t.m.bank(1)[:, b:b + 1], t.m.alpha[:, b, :], ones[:, 0:1],
                                   start=True, stop=True)
                mm.then_inc(rsum_mm, 1)

            def a_rt(t):
                pe.wait_ge(rrec_ready, t.at(1))
                for b in range(G):
                    mm = pe.transpose(t.m.quarter(1, b), t.m.rrec[:, b:b + 1].broadcast_to([P, P]), ident[:])
                mm.then_inc(rt_mm, 1)

            def a_xw0(t, b):
                pe.wait_ge(zsum_ready, t.at(1))
                if b == 2:
                    pe.wait_ge(trans_ready, t.at(1))
                dst = t.m.half(b // 2, b % 2)
                pe.matmul(dst, ones_r[:], row[:], start=(b % 2 == 0), stop=False, skip_group_check=True)
                mm = rows_times(dst, t.m.xa_hi, t.m.xa_lo, b, W_H, D, False, False)
                if b == G - 1:
                    mm.then_inc(xw0_mm, 1)

            def a_ty2(t):
                pe.wait_ge(trans_ready, t.at(1))
                for b in range(G):
                    mm = pe.matmul(t.m.half(2 + b // 2, b % 2), t.m.trans[:, b, :], t.m.y2[:, b, 0:D],
                                   start=False, stop=True, skip_group_check=True)
                    if b % 2:
                        mm.then_inc(zed_mm, 1)

            def a_tz(t):
                for p in range(PAIRS):
                    pe.wait_ge(zed_ready, t.at(2, p + 1))
                    for j in range(2):
                        b = 2 * p + j
                        mm = pe.matmul(t.m.half(p, j), t.m.trans[:, b, :], t.m.zed[:, b, :],
                                       start=False, stop=True, skip_group_check=True)
                    mm.then_inc(h_mm, 1)

            def a_x1t(t):
                turn_rows(t, t.m.x1, 0, 2, x1t_mm)

            def a_xpt(t, m):
                for c in range(C):
                    if m == 0:
                        pe.wait_ge(x1_hi_ready, t.at(2, c + 1))
                        pe.wait_ge(x1_lo_ready, t.at(2, c + 1))
                    w = W_P + c * D + m * P
                    mm = product(t.m.bank(m), (w_hi[:, w:w + P], w_lo[:, w:w + P]),
                                 (t.m.x1_hi[:, c], t.m.x1_lo[:, c]), c == 0, c == C - 1)
                mm.then_inc(xpt_mm, 1)

            def a_xp(t):
                pe.wait_ge(xpt_ready, t.at(2))
                for b in range(G):
                    for c in range(C):
                        mm = pe.transpose(t.m.half(2 + b // 2, b % 2)[:, c * P:(c + 1) * P],
                                          t.m.xp_t[:, c, b, :], ident[:])
                    if b % 2:
                        mm.then_inc(xp_mm, 1)

            def a_xct(t, c):
                pe.wait_ge(xpt_ready, t.at(2))
                pe.matmul(t.m.bank(c), c_t[:, c, :], t.m.xp_t[:, c], start=True, stop=True).then_inc(xct_mm, 1)

            def a_scores(t, p, k):
                if p == 0:
                    pe.wait_ge(xct_ready, t.at(2))
                    if k:
                        pe.wait_ge(xp_ready, t.at(2))
                else:
                    pe.wait_ge(score_ready, t.at(4, k + 1))
                for c in range(C):
                    for j in range(2):
                        for q in (2 * k, 2 * k + 1):
                            rows_q = slice(DH * q, DH * q + DH)
                            mm = pe.matmul(t.m.quarter(q, 2 * c + j),
                                           t.m.xp_t[rows_q, c, 2 * p + j, :], t.m.xc_t[rows_q, c, 2 * p + j, :],
                                           start=True, stop=True)
                mm.then_inc(score_mm, 1)

            def a_xh(t, b):
                p, j = b // 2, b % 2
                pe.wait_ge(attn_ready, t.at(4, 2 * p + 2))
                if b == 0:
                    pe.wait_ge(score_ready, t.at(4, 3))
                for h in range(H):
                    mm = pe.matmul(t.m.half(p, j)[:, h * DH:(h + 1) * DH],
                                   t.m.attn[:, p, h % QH, h // QH, j, :],
                                   t.m.xp[:, b, h * DH:(h + 1) * DH], start=True, stop=True)
                if j:
                    mm.then_inc(xh_mm, 1)

            def b_x2t(t, before):
                if before:
                    pe.wait_ge(h2_ready, before.at(2))
                turn_rows(t, x2, 1, 0, x2t_mm)

            def b_qkv(t, b, before):
                pe.wait_ge(x2_hi_ready, t.at(2))
                pe.wait_ge(x2_lo_ready, t.at(2))
                if b >= 2 and before:
                    pe.wait_ge(y_ready[3], before.at(2))
                rows_times(t.m.ps[:, b, 0:QKVW], t.m.x2_hi, t.m.x2_lo, b, W_QKV, QKVW, True, True)\
                    .then_inc(qkv_mm, 1)

            def c_ak(t):
                pe.wait_ge(qk_ready, t.at(1))
                if not t.m.spare:
                    pe.wait_ge(adj_c_loaded, t.at(16))
                for b in range(G):
                    mm = pe.matmul(t.m.ps[:, b, QKVW:QKVW + E], t.m.adj[:, b, :], t.m.qk[:, b, E:QK],
                                   start=True, stop=True)
                mm.then_inc(ak_mm, 1)

            def c_wt(t):
                pe.wait_ge(wsum_ready, t.at(1))
                pe.matmul(t.m.ps[0:G, 0, D:D + P], t.m.wsum[:], ident[:], start=True, stop=True).then_inc(wt_mm, 1)

            def c_wcol(t):
                pe.wait_ge(wnorm_ready, t.at(1))
                pe.matmul(t.m.ps[:, 1, D:D + G], t.m.wnorm[:], ident[0:G, 0:G], start=True, stop=True)\
                  .then_inc(wcol_mm, 1)

            def c_x3t(t):
                turn_rows(t, t.m.x3, 2, 0, x3t_mm)

            def c_s1(t, c):
                pe.wait_ge(x3_hi_ready, t.at(2, c + 1))
                pe.wait_ge(x3_lo_ready, t.at(2, c + 1))
                for b in range(G):
                    mm = product(t.m.half(2 + b // 2, b % 2), split(t.m.x3_hi, t.m.x3_lo, c, b),
                                 weights(W_S1, D, c), c == 0 and b % 2 == 0, c == C - 1)
                    if c == C - 1 and b % 2:
                        mm.then_inc(s1_mm, 1)

            def gcn_turn(t, s, s_ready, done):
                for p in range(PAIRS):
                    pe.wait_ge(s_ready, t.at(2, p + 1))
                    for c in range(C):
                        for b in (2 * p, 2 * p + 1):
                            mm = pe.matmul(t.m.quarter(c, b), s[:, b, c * P:(c + 1) * P], t.m.adj[:, b, :],
                                           start=True, stop=True)
                        if p == PAIRS - 1:
                            mm.then_inc(done, 1)

            def high_rows(t, c, at, hi_ready):
                pe.wait_ge(hi_ready, t.at(2, c + 1))
                w_high, w_low = weights(at, D, c)
                for b in range(G):
                    dst, h = t.m.half(2 + b // 2, b % 2), t.m.h_hi[:, c, b, :]
                    pe.matmul(dst, h, w_low, start=(c == 0 and b % 2 == 0), stop=False, skip_group_check=True)
                    pe.matmul(dst, h, w_high, start=False, stop=False, skip_group_check=True)

            def low_rows(t, at, lo_ready, done):
                for c in range(C):
                    pe.wait_ge(lo_ready, t.at(2, c + 1))
                    for b in range(G):
                        mm = pe.matmul(t.m.half(2 + b // 2, b % 2), t.m.h_lo[:, c, b, :], weights(at, D, c)[0],
                                       start=False, stop=(c == C - 1), skip_group_check=True)
                        if c == C - 1 and b % 2:
                            mm.then_inc(done, 1)

            def c_s2_hi(t, c):
                high_rows(t, c, W_S2, h1_hi_ready)

            def c_s2_lo(t):
                low_rows(t, W_S2, h1_lo_ready, s2_mm)

            def c_s3(t, b):
                pe.wait_ge(h2_hi_ready, t.at(2))
                pe.wait_ge(h2_lo_ready, t.at(2))
                mm = rows_times(t.m.half(2 + b // 2, b % 2), t.m.h_hi, t.m.h_lo, b, W_S3, D, True, True)
                if b % 2:
                    mm.then_inc(s3_mm, 1)

            def c_out(t, p):
                pe.wait_ge(s3_ready, t.at(2, p + 1))
                for b in (2 * p, 2 * p + 1):
                    mm = pe.matmul(t.m.half(2 + p, b % 2), t.m.adj[:, b, :], t.m.s[:, b, :],
                                   start=True, stop=True)
                mm.then_inc(o_mm, 1)

            pe.wait_ge(wva_loaded, 16 * len(wva_loads))
            for m in range(C):
                for c in range(C):
                    mm = pe.matmul(ps[:, 0, 2 * m:2 * m + 2], wv_t[:, c, m * P:(m + 1) * P], aw_c[:, :, c],
                                   start=(c == 0), stop=(c == C - 1))
            for c in range(C):
                mm = pe.matmul(ps[:, 1, 0:2], bv_c[:, c:c + 1].broadcast_to([P, P]), aw_c[:, :, c],
                               start=(c == 0), stop=(c == C - 1))
            mm.then_inc(wva_mm, 1)
            pe.wait_ge(consts, CONSTS)
            pe.wait_ge(ident_ready, 1)

            def has_weights(n):
                pe.wait_ge(w_hi_ready, n + 1)
                pe.wait_ge(w_lo_ready, n + 1)

            def head():
                a0, a1, b0 = Turn(pe, 0, A_LANE), Turn(pe, 1, A_SPARE), Turn(pe, 0, C_LANE)
                a2 = Turn(pe, 2, A_LANE, first=True)
                has_weights(0)
                a_y2(a0, 1)
                a_y2(a0, 0)
                a_si(a0)
                has_weights(1)
                a_xw1(a0, 0)
                a_xw1(a0, 1)
                a_y2(a1, 1)
                a_y2(a1, 0)
                a_xw1(a0, 2)
                a_rsum(a0)
                a_xw1(a0, 3)
                a_rt(a0)
                a_si(a1)
                has_weights(2)
                pe.wait_ge(row_moved, 16)
                a_xw0(a0, 0)
                a_xw0(a0, 1)
                a_ty2(a0)
                a_xw0(a0, 2)
                a_xw0(a0, 3)
                a_xw1(a1, 0)
                a_rsum(a1)
                a_tz(a0)
                a_xw1(a1, 1)
                a_rt(a1)
                a_xw1(a1, 2)
                a_xw1(a1, 3)
                a_xw0(a1, 0)
                a_xw0(a1, 1)
                a_ty2(a1)
                a_xw0(a1, 2)
                a_xw0(a1, 3)
                a_tz(a1)
                a_x1t(a0)
                has_weights(3)
                a_xpt(a0, 0)
                a_xpt(a0, 1)
                a_x1t(a1)
                a_xp(a0)
                pe.wait_ge(c_loaded, 16 * H)
                a_xct(a0, 0)
                a_xct(a0, 1)
                a_xpt(a1, 0)
                a_scores(a0, 0, 0)
                a_scores(a0, 0, 1)
                a_scores(a0, 1, 0)
                a_xpt(a1, 1)
                a_xp(a1)
                a_scores(a0, 1, 1)
                a_xh(a0, 0)
                a_xh(a0, 1)
                a_xct(a1, 0)
                a_xh(a0, 2)
                pe.wait_ge(score_ready, a0.at(4))
                a_y2(a2, 1)
                a_xct(a1, 1)
                a_xh(a0, 3)
                a_scores(a1, 0, 0)
                a_xw1(a2, 0)
                a_scores(a1, 0, 1)
                pe.wait_ge(y_ready[1], a0.at(2))
                a_y2(a2, 0)
                a_scores(a1, 1, 0)
                a_scores(a1, 1, 1)
                a_xw1(a2, 1)
                pe.wait_ge(score_ready, a1.at(4))
                b_x2t(b0, None)
                a_xw1(a2, 2)
                a_xh(a1, 0)
                a_xh(a1, 1)
                a_xh(a1, 2)
                has_weights(4)
                b_qkv(b0, 0, None)
                a_xh(a1, 3)
                b_qkv(b0, 1, None)
                pe.wait_ge(y_ready[1], a1.at(2))
                b_qkv(b0, 2, None)
                b_qkv(b0, 3, None)
                has_weights(len(sections) - 1)

            def body(g, opened=False):
                a, b, c = Turn(pe, g, A_LANE), Turn(pe, g - 1, C_LANE), Turn(pe, g - 2, C_LANE)
                if not opened:
                    a_y2(a, 1)
                c_ak(c)
                if not opened:
                    a_y2(a, 0)
                c_wt(c)
                a_si(a)
                if not opened:
                    a_xw1(a, 0)
                    a_xw1(a, 1)
                    a_xw1(a, 2)
                a_xw1(a, 3)
                c_wcol(c)
                a_rsum(a)
                a_xw0(a, 0)
                a_rt(a)
                a_xw0(a, 1)
                a_ty2(a)
                a_xw0(a, 2)
                a_xw0(a, 3)
                c_x3t(c)
                a_tz(a)
                c_s1(c, 0)
                c_s1(c, 1)
                gcn_turn(c, c.m.s, s1_ready, h1_mm)
                c_s2_hi(c, 0)
                c_s2_hi(c, 1)
                a_x1t(a)
                c_s2_lo(c)
                a_xpt(a, 0)
                a_xpt(a, 1)
                gcn_turn(c, c.m.s, s2_ready, h2_mm)
                a_xp(a)
                a_xct(a, 0)
                a_xct(a, 1)
                b_x2t(b, c)
                a_scores(a, 0, 0)
                c_s3(c, 0)
                a_scores(a, 0, 1)
                c_s3(c, 1)
                a_scores(a, 1, 0)
                c_s3(c, 2)
                a_scores(a, 1, 1)
                c_s3(c, 3)
                a_xh(a, 0)
                c_out(c, 0)
                a_xh(a, 1)
                c_out(c, 1)
                a_xh(a, 2)
                b_qkv(b, 0, c)
                a_xh(a, 3)
                b_qkv(b, 1, c)
                b_qkv(b, 2, c)
                b_qkv(b, 3, c)

            def tail():
                c, d = Turn(pe, GROUPS - 2, C_LANE), Turn(pe, GROUPS - 1, C_SPARE)
                c_ak(c)
                b_x2t(d, None)
                c_wt(c)
                b_qkv(d, 0, None)
                c_wcol(c)
                b_qkv(d, 1, None)
                b_qkv(d, 2, None)
                b_qkv(d, 3, None)
                c_ak(d)
                c_x3t(c)
                c_wt(d)
                c_s1(c, 0)
                c_wcol(d)
                c_s1(c, 1)
                gcn_turn(c, c.m.s, s1_ready, h1_mm)
                c_s2_hi(c, 0)
                c_s2_hi(c, 1)
                c_x3t(d)
                c_s2_lo(c)
                c_s1(d, 0)
                gcn_turn(c, c.m.s, s2_ready, h2_mm)
                c_s1(d, 1)
                gcn_turn(d, d.m.s, s1_ready, h1_mm)
                for b in range(G):
                    c_s3(c, b)
                c_s2_hi(d, 0)
                c_s2_hi(d, 1)
                c_out(c, 0)
                c_s2_lo(d)
                c_out(c, 1)
                gcn_turn(d, d.m.s, s2_ready, h2_mm)
                high_rows(d, 0, W_S3, h2_hi_ready)
                high_rows(d, 1, W_S3, h2_hi_ready)
                low_rows(d, W_S3, h2_lo_ready, s3_mm)
                c_out(d, 0)
                c_out(d, 1)

            head()
            body(2, opened=True)
            with pe.Fori(3, GROUPS) as g:
                body(g)
            tail()

        @block.scalar
        def _(act):
            copy, exp, ident_f = ACT.Copy, ACT.Exp, ACT.Identity

            def split_weights(n):
                a, b = sections[n]
                act.wait_ge(w_loaded[n], 16)
                if n == 0:
                    act.wait_ge(wva_sb, 1)
                act.activation(w_hi[:, a:b], w_raw[:, a:b], copy).then_inc(w_hi_ready, 1)

            def hi_part(dst, first, mm, ready, t):
                for c in range(C):
                    act.wait_ge(mm, t.at(2, c + 1))
                    act.activation(dst[:, c], t.m.bank(first + c), copy).then_inc(ready, 1)

            def rows_pair(dst, first, mm, ready, t, p):
                act.wait_ge(mm, t.at(2, p + 1))
                act.activation(dst[:, 2 * p:2 * p + 2, :], t.m.bank(first + p), copy).then_inc(ready, 1)

            def rows(dst, first, mm, ready, t):
                for p in range(PAIRS):
                    rows_pair(dst, first, mm, ready, t, p)

            def relu_of(dst, bias, mm, ready, t):
                for c in range(C):
                    act.wait_ge(mm, t.at(2, c + 1))
                    act.activation(dst[:, c], t.m.bank(c), ACT.Relu, bias=bias[:, c:c + 1]).then_inc(ready, 1)

            def a_y2(t, p):
                act.wait_ge(y2_mm, t.at(2, 2 - p))
                act.activation(t.m.y2[:, 2 * p:2 * p + 2, :], t.m.two(2 * p)[:, :, 0:Y2W], copy)\
                   .then_inc(y2_ready, 1)

            def a_exp(t):
                act.wait_ge(zrelu_ready, t.at(1))
                act.activation(t.m.zexp[:], t.m.zrelu[:], exp).then_inc(zexp_ready, 1)

            def a_xpt(t, m):
                act.wait_ge(xpt_mm, t.at(2, m + 1))
                act.activation(t.m.xp_t[:, m], t.m.bank(m), ident_f, bias=bp_c[:, m:m + 1])\
                   .then_inc(xpt_ready, 1)

            def a_xct(t):
                for m in range(C):
                    act.wait_ge(xct_mm, t.at(2, m + 1))
                    act.activation(t.m.xc_t[:, m], t.m.bank(m), copy).then_inc(xct_ready, 1)

            def a_tanh(t, p, k):
                q = slice(2 * k, 2 * k + 2)
                act.wait_ge(score_ready, t.at(4, 2 * p + k + 1))
                act.activation(t.m.attn[:, p, q], t.m.attn[:, p, q], ACT.Tanh).then_inc(attn_ready, 1)

            def b_x2(t):
                hi_part(t.m.x2_hi, 0, x2t_mm, x2_hi_ready, t)
                if not t.first:
                    act.wait_ge(y_ready[2], t.at(2, 0))
                act.activation(t.m.x2_kept[:], x2[:], copy).then_inc(x2_kept_ready, 1)

            def b_qk(t):
                act.wait_ge(qkv_mm, t.at(4))
                act.activation(t.m.qk[:], t.m.ps[:, :, D:QKVW], copy).then_inc(qk_ready, 1)

            def c_exp(t):
                act.wait_ge(wbias_ready, t.at(1))
                act.activation(t.m.wexp[:], t.m.ps[0:G, 0, D:D + P], exp, bias=t.m.wbias[:], scale=E ** -0.5,
                               accum_out=t.m.wden[:]).then_inc(wexp_ready, 1)

            def head():
                act.wait_ge(seed_ready, 1)
                act.activation(act_seed[:], act_seed[:], exp).then_inc(seed_ready, 1)
                a0, a1, b0 = Turn(act, 0, A_LANE), Turn(act, 1, A_SPARE), Turn(act, 0, C_LANE)
                a2 = Turn(act, 2, A_LANE)
                act.wait_ge(xt_loaded, a0.at(16))
                act.activation(a0.m.xa_hi[:], a0.m.xa_t[:], copy).then_inc(xa_hi_ready, 1)
                split_weights(0)
                act.wait_ge(row_sum, 2)
                act.activation(row[0:1], row_raw[:], copy).then_inc(row_hi_ready, 1)
                split_weights(1)
                a_y2(a0, 1)
                a_y2(a0, 0)
                split_weights(2)
                a_exp(a0)
                split_weights(3)
                a_y2(a1, 1)
                a_y2(a1, 0)
                a_exp(a1)
                rows(a0.m.zed, 2, zed_mm, zed_ready, a0)
                for n in range(4, 8):
                    split_weights(n)
                rows(a1.m.zed, 2, zed_mm, zed_ready, a1)
                act.wait_ge(rest_loaded, 16 * len(rest_loads))
                hi_part(a0.m.x1_hi, 2, x1t_mm, x1_hi_ready, a0)
                a_xpt(a0, 0)
                a_xpt(a0, 1)
                hi_part(a1.m.x1_hi, 2, x1t_mm, x1_hi_ready, a1)
                a_xct(a0)
                a_tanh(a0, 0, 0)
                a_tanh(a0, 0, 1)
                a_xpt(a1, 0)
                a_tanh(a0, 1, 0)
                a_xpt(a1, 1)
                a_tanh(a0, 1, 1)
                a_y2(a2, 1)
                a_xct(a1)
                a_tanh(a1, 0, 0)
                a_y2(a2, 0)
                a_tanh(a1, 0, 1)
                a_tanh(a1, 1, 0)
                a_tanh(a1, 1, 1)
                b_x2(b0)
                b_qk(b0)

            def body(g, opened=False):
                a, b, c = Turn(act, g, A_LANE), Turn(act, g - 1, C_LANE), Turn(act, g - 2, C_LANE)
                if not opened:
                    a_y2(a, 1)
                    a_y2(a, 0)
                c_exp(c)
                a_exp(a)
                rows(a.m.zed, 2, zed_mm, zed_ready, a)
                hi_part(c.m.x3_hi, 0, x3t_mm, x3_hi_ready, c)
                rows(c.m.s, 2, s1_mm, s1_ready, c)
                relu_of(c.m.h_hi, b1_c, h1_mm, h1_hi_ready, c)
                hi_part(a.m.x1_hi, 2, x1t_mm, x1_hi_ready, a)
                rows(c.m.s, 2, s2_mm, s2_ready, c)
                a_xpt(a, 0)
                a_xpt(a, 1)
                relu_of(c.m.h_hi, b2_c, h2_mm, h2_hi_ready, c)
                a_xct(a)
                b_x2(b)
                a_tanh(a, 0, 0)
                a_tanh(a, 0, 1)
                rows_pair(c.m.s, 2, s3_mm, s3_ready, c, 0)
                a_tanh(a, 1, 0)
                rows_pair(c.m.s, 2, s3_mm, s3_ready, c, 1)
                a_tanh(a, 1, 1)
                b_qk(b)

            def tail():
                c, d = Turn(act, GROUPS - 2, C_LANE), Turn(act, GROUPS - 1, C_SPARE)
                b_x2(d)
                c_exp(c)
                b_qk(d)
                hi_part(c.m.x3_hi, 0, x3t_mm, x3_hi_ready, c)
                c_exp(d)
                rows(c.m.s, 2, s1_mm, s1_ready, c)
                relu_of(c.m.h_hi, b1_c, h1_mm, h1_hi_ready, c)
                hi_part(d.m.x3_hi, 0, x3t_mm, x3_hi_ready, d)
                rows(c.m.s, 2, s2_mm, s2_ready, c)
                relu_of(c.m.h_hi, b2_c, h2_mm, h2_hi_ready, c)
                rows(d.m.s, 2, s1_mm, s1_ready, d)
                relu_of(d.m.h_hi, b1_c, h1_mm, h1_hi_ready, d)
                rows(c.m.s, 2, s3_mm, s3_ready, c)
                rows(d.m.s, 2, s2_mm, s2_ready, d)
                relu_of(d.m.h_hi, b2_c, h2_mm, h2_hi_ready, d)
                rows(d.m.s, 2, s3_mm, s3_ready, d)

            head()
            body(2, opened=True)
            with act.Fori(3, GROUPS) as g:
                body(g)
            tail()

        @block.vector
        def _(dve):
            def lo_of_weights(n):
                a, b = sections[n]
                dve.wait_ge(w_hi_ready, n + 1)
                dve.tensor_tensor(w_lo[:, a:b], w_raw[:, a:b], w_hi[:, a:b].bitcast(F32), ALU.subtract)\
                   .then_inc(w_lo_ready, 1)

            def lo_part(dst, hi, first, hi_ready, ready, t):
                for c in range(C):
                    dve.wait_ge(hi_ready, t.at(2, c + 1))
                    dve.tensor_tensor(dst[:, c], t.m.bank(first + c), hi[:, c].bitcast(F32), ALU.subtract)\
                       .then_inc(ready, 1)

            def norm_stats(n, y, t):
                st, mv = t.m.st[n], t.m.mv[n]
                dve.wait_ge(y_ready[n], t.at(2))
                for b in range(G):
                    op = dve.bn_stats(st[:, b, :], y[:, b, :])
                op.then_inc(st_ready[n], 1)
                dve.wait_ge(st_ready[n], t.at(1))
                dve.memset(t.m.anchor[n][:], 0.0)
                for b in range(G):
                    op = dve.bn_aggr(mv[:, b, :], st[:, b, :])
                op.then_inc(mv_ready[n], 1)
                dve.wait_ge(mv_ready[n], t.at(1))
                dve.tensor_scalar(t.m.ve[n][:], mv[:, :, 1], EPS, None, ALU.add).then_inc(ve_ready[n], 1)

            def norm_rows(n, y, dst, t, graphs=range(G)):
                dve.wait_ge(rs_ready[n], t.at(1))
                for b in graphs:
                    op = dve.tensor_scalar(dst[:, b, :], y[:, b, :], t.m.mv[n][:, b, 0:1],
                                           t.m.rs[n][:, b:b + 1], ALU.subtract, ALU.mult)
                    if b % 2:
                        op.then_inc(x_ready[n], 1)

            def a_sum(n, mm, x_in, t, p):
                dve.wait_ge(mm, t.at(2, p + 1))
                pair = slice(2 * p, 2 * p + 2)
                dve.scalar_tensor_tensor(t.m.ya[:, pair, :], t.m.bank(p), 0.0, x_in[:, pair, :],
                                         ALU.max, ALU.add).then_inc(y_ready[n], 1)

            def a_z(t):
                m = t.m
                dve.wait_ge(si_mm, t.at(1))
                dve.scalar_tensor_tensor(m.zsum[:], m.bank(0).rearrange("p (b n) -> p b n", b=G), z_const[:, 0:1],
                                         m.y2[:, :, D:D + 1].broadcast_to([P, G, P]),
                                         ALU.add, ALU.add).then_inc(zsum_ready, 1)
                dve.wait_ge(zsum_ready, t.at(1))
                dve.scalar_tensor_tensor(m.zrelu[:], m.zsum[:], SLOPE, m.zsum[:], ALU.mult, ALU.max)\
                   .then_inc(zrelu_ready, 1)

            def a_alpha(t):
                dve.wait_ge(adj_a_loaded, t.at(16))
                dve.wait_ge(zexp_ready, t.at(1))
                dve.tensor_tensor(t.m.alpha[:], t.m.adj[:], t.m.zexp[:], ALU.mult).then_inc(alpha_ready, 1)

            def a_rrec(t):
                dve.wait_ge(rsum_mm, t.at(1))
                dve.tensor_scalar(t.m.rsum[:], t.m.bank(1)[:, 0:G], TINY, None, ALU.add).then_inc(rsum_ready, 1)
                dve.wait_ge(rsum_ready, t.at(1))
                dve.reciprocal(t.m.rrec[:], t.m.rsum[:]).then_inc(rrec_ready, 1)

            def a_trans(t):
                dve.wait_ge(rt_mm, t.at(1))
                dve.tensor_tensor(t.m.trans[:], t.m.alpha[:], t.m.bank(1).rearrange("p (b n) -> p b n", b=G),
                                  ALU.mult).then_inc(trans_ready, 1)

            def a_sum0(t):
                dve.wait_ge(x_loaded, t.at(16))
                a_sum(0, h_mm, t.m.xa, t, 0)
                a_sum(0, h_mm, t.m.xa, t, 1)

            def a_x1_lo(t):
                lo_part(t.m.x1_lo, t.m.x1_hi, 2, x1_hi_ready, x1_lo_ready, t)

            def a_xp(t):
                for p in range(PAIRS):
                    dve.wait_ge(xp_mm, t.at(2, p + 1))
                    dve.tensor_copy(t.m.xp[:, 2 * p:2 * p + 2, :], t.m.bank(2 + p)).then_inc(xp_ready, 1)

            def a_scores(t, p, k):
                dve.wait_ge(score_mm, t.at(4, 2 * p + k + 1))
                pair = t.m.adj[:, 2 * p:2 * p + 2, :].rearrange("p b n -> p (b n)")
                dve.tensor_tensor(
                    t.m.attn[:, p, 2 * k:2 * k + 2].rearrange("p q c b n -> p (q c) (b n)"),
                    t.m.two(2 * k).rearrange("p q (c m) -> p (q c) m", c=C),
                    pair.unsqueeze(1).broadcast_to([P, 2 * C, 2 * P]), ALU.mult).then_inc(score_ready, 1)

            def b_x2_lo(t):
                lo_part(t.m.x2_lo, t.m.x2_hi, 0, x2_hi_ready, x2_lo_ready, t)

            def c_wsum(t):
                m = t.m
                dve.wait_ge(ak_mm, t.at(1))
                dve.tensor_tensor(m.qak[:], m.qk[:, :, 0:E], m.ps[:, :, QKVW:QKVW + E], ALU.mult)\
                   .then_inc(qak_ready, 1)
                dve.wait_ge(qak_ready, t.at(1))
                dve.reduce_sum(m.wsum[:], m.qak[:], AX_X).then_inc(wsum_ready, 1)

            def c_wmax(t):
                m = t.m
                dve.wait_ge(wt_mm, t.at(1))
                dve.reduce_max(m.wmax[:], m.ps[0:G, 0, D:D + P], AX_X).then_inc(wmax_ready, 1)
                dve.wait_ge(wmax_ready, t.at(1))
                dve.tensor_scalar(m.wbias[:], m.wmax[:], -E ** -0.5, None, ALU.mult).then_inc(wbias_ready, 1)

            def c_wnorm(t):
                m = t.m
                dve.wait_ge(wexp_ready, t.at(1))
                dve.reciprocal(m.wrec[:], m.wden[:]).then_inc(wrec_ready, 1)
                dve.wait_ge(wrec_ready, t.at(1))
                dve.tensor_scalar(m.wnorm[:], m.wexp[:], m.wrec[:, 0:1], None, ALU.mult).then_inc(wnorm_ready, 1)

            def c_wcol(t):
                dve.wait_ge(wcol_mm, t.at(1))
                dve.tensor_copy(t.m.wcol[:], t.m.ps[:, 1, D:D + G]).then_inc(wcol_ready, 1)

            def c_weigh(t, p):
                m = t.m
                if p == 0:
                    dve.wait_ge(x2_kept_ready, t.at(1))
                    dve.wait_ge(wcol_ready, t.at(1))
                for b in (2 * p, 2 * p + 1):
                    op = dve.scalar_tensor_tensor(m.yb[:, b, :], m.ps[:, b, 0:D], m.wcol[:, b:b + 1],
                                                  m.x2_kept[:, b, :], ALU.mult, ALU.add)
                op.then_inc(y_ready[2], 1)

            def c_x3_lo(t):
                lo_part(t.m.x3_lo, t.m.x3_hi, 0, x3_hi_ready, x3_lo_ready, t)

            def relu_of(bias, hi_ready, ready, t, c):
                dve.wait_ge(hi_ready, t.at(2, c + 1))
                dve.tensor_scalar(t.m.h_t[:, c], t.m.bank(c), bias[:, c:c + 1], 0.0, ALU.add, ALU.max)\
                   .then_inc(ready, 1)

            def relu_lo(ready, lo_ready, t, c):
                dve.wait_ge(ready, t.at(2, c + 1))
                dve.tensor_tensor(t.m.h_lo[:, c], t.m.h_t[:, c], t.m.h_hi[:, c].bitcast(F32), ALU.subtract)\
                   .then_inc(lo_ready, 1)

            def c_h1(t):
                for c in range(C):
                    relu_of(b1_c, h1_hi_ready, h1_ready, t, c)
                    relu_lo(h1_ready, h1_lo_ready, t, c)

            def c_h2(t):
                for c in range(C):
                    relu_of(b2_c, h2_hi_ready, h2_ready, t, c)

            def c_h2_lo(t):
                for c in range(C):
                    relu_lo(h2_ready, h2_lo_ready, t, c)

            def c_sum(t):
                dve.wait_ge(x3b_ready, t.at(1))
                for p in range(PAIRS):
                    dve.wait_ge(o_mm, t.at(2, p + 1))
                    pair = slice(2 * p, 2 * p + 2)
                    dve.tensor_tensor(t.m.yo[:, pair, :], t.m.bank(2 + p), t.m.x3b[:, pair, :], ALU.add)\
                       .then_inc(y_ready[3], 1)

            def c_x4(t):
                if not t.first:
                    dve.wait_ge(stored, t.at(16, 0))
                norm_rows(3, t.m.yo, t.m.x4, t)

            def head():
                a0, a1, b0 = Turn(dve, 0, A_LANE), Turn(dve, 1, A_SPARE), Turn(dve, 0, C_LANE)
                dve.wait_ge(wva_mm, 1)
                for m in range(C):
                    a = W_Y2 + m * Y2W + D
                    cp = dve.tensor_copy(w_raw[:, a:a + 2], ps[:, 0, 2 * m:2 * m + 2])
                cp.then_inc(wva_sb, 1)
                dve.tensor_copy(z_bias[:], ps[:, 1, 0:2]).then_inc(zb_sb, 1)
                dve.wait_ge(xa_hi_ready, a0.at(1))
                dve.tensor_tensor(a0.m.xa_lo[:], a0.m.xa_t[:], a0.m.xa_hi[:].bitcast(F32), ALU.subtract)\
                   .then_inc(xa_lo_ready, 1)
                lo_of_weights(0)
                dve.wait_ge(bias_loaded, 16 * len(bias_loads))
                dve.tensor_tensor(row_raw[:], bk_row[:, 0, :], bk_row[:, 1, :], ALU.add).then_inc(row_sum, 1)
                dve.wait_ge(zb_sb, 1)
                dve.scalar_tensor_tensor(z_const[:], z_bias[:, 0:1], ab_c[:, 0:1], z_bias[:, 1:2],
                                         ALU.add, ALU.add).then_inc(z_const_ready, 1)
                dve.wait_ge(row_sum, 1)
                dve.tensor_tensor(row_raw[:], row_raw[:], bk_row[:, 2, :], ALU.add).then_inc(row_sum, 1)
                lo_of_weights(1)
                dve.wait_ge(row_hi_ready, 1)
                dve.tensor_tensor(row_lo[:], row_raw[:], row[0:1].bitcast(F32), ALU.subtract)\
                   .then_inc(row_lo_ready, 1)
                dve.wait_ge(z_const_ready, 1)
                a_z(a0)
                lo_of_weights(2)
                a_alpha(a0)
                a_rrec(a0)
                a_trans(a0)
                a_z(a1)
                lo_of_weights(3)
                a_alpha(a1)
                a_rrec(a1)
                a_sum0(a0)
                norm_stats(0, a0.m.ya, a0)
                a_trans(a1)
                lo_of_weights(4)
                norm_rows(0, a0.m.ya, a0.m.x1, a0)
                lo_of_weights(5)
                lo_of_weights(6)
                dve.wait_ge(w_lo_ready, 7)
                a_sum0(a1)
                a_x1_lo(a0)
                norm_stats(0, a1.m.ya, a1)
                lo_of_weights(7)
                norm_rows(0, a1.m.ya, a1.m.x1, a1)
                a_xp(a0)
                a_x1_lo(a1)
                a_scores(a0, 0, 0)
                a_scores(a0, 0, 1)
                a_scores(a0, 1, 0)
                a_scores(a0, 1, 1)
                a_xp(a1)
                a_sum(1, xh_mm, a0.m.x1, a0, 0)
                a_sum(1, xh_mm, a0.m.x1, a0, 1)
                norm_stats(1, a0.m.ya, a0)
                a_scores(a1, 0, 0)
                norm_rows(1, a0.m.ya, x2, a0)
                a_scores(a1, 0, 1)
                a_scores(a1, 1, 0)
                a_scores(a1, 1, 1)
                b_x2_lo(b0)
                a_sum(1, xh_mm, a1.m.x1, a1, 0)
                a_sum(1, xh_mm, a1.m.x1, a1, 1)
                norm_stats(1, a1.m.ya, a1)

            def body(g, lane_before=A_LANE):
                a, b, c = Turn(dve, g, A_LANE), Turn(dve, g - 1, C_LANE), Turn(dve, g - 2, C_LANE)
                before = Turn(dve, g - 1, lane_before)
                c_wsum(c)
                c_wmax(c)
                a_z(a)
                c_wnorm(c)
                a_alpha(a)
                c_wcol(c)
                c_weigh(c, 0)
                a_rrec(a)
                c_weigh(c, 1)
                a_trans(a)
                norm_stats(2, c.m.yb, c)
                norm_rows(1, before.m.ya, x2, before, (0, 1))
                norm_rows(2, c.m.yb, c.m.x3, c)
                norm_rows(1, before.m.ya, x2, before, (2, 3))
                c_x3_lo(c)
                dve.wait_ge(x_ready[1], before.at(2))
                a_sum0(a)
                norm_stats(0, a.m.ya, a)
                norm_rows(0, a.m.ya, a.m.x1, a, (0, 1))
                relu_of(b1_c, h1_hi_ready, h1_ready, c, 0)
                norm_rows(0, a.m.ya, a.m.x1, a, (2, 3))
                relu_of(b1_c, h1_hi_ready, h1_ready, c, 1)
                relu_lo(h1_ready, h1_lo_ready, c, 0)
                relu_lo(h1_ready, h1_lo_ready, c, 1)
                a_x1_lo(a)
                c_h2(c)
                a_xp(a)
                c_h2_lo(c)
                b_x2_lo(b)
                for n in range(4):
                    a_scores(a, n // 2, n % 2)
                c_sum(c)
                norm_stats(3, c.m.yo, c)
                a_sum(1, xh_mm, a.m.x1, a, 0)
                c_x4(c)
                a_sum(1, xh_mm, a.m.x1, a, 1)
                norm_stats(1, a.m.ya, a)

            def tail():
                c, d = Turn(dve, GROUPS - 2, C_LANE), Turn(dve, GROUPS - 1, C_SPARE)
                last = Turn(dve, GROUPS - 1, A_LANE)
                dve.wait_ge(x2_kept_ready, c.at(1))
                norm_rows(1, last.m.ya, x2, last)
                c_wsum(c)
                c_wmax(c)
                b_x2_lo(d)
                c_wnorm(c)
                c_wcol(c)
                c_weigh(c, 0)
                c_weigh(c, 1)
                norm_stats(2, c.m.yb, c)
                c_wsum(d)
                norm_rows(2, c.m.yb, c.m.x3, c)
                c_x3_lo(c)
                c_wmax(d)
                c_wnorm(d)
                c_wcol(d)
                c_weigh(d, 0)
                c_weigh(d, 1)
                norm_stats(2, d.m.yb, d)
                c_h1(c)
                norm_rows(2, d.m.yb, d.m.x3, d)
                c_x3_lo(d)
                c_h2(c)
                c_h2_lo(c)
                c_h1(d)
                c_sum(c)
                norm_stats(3, c.m.yo, c)
                for n in range(C):
                    relu_of(b2_c, h2_hi_ready, h2_ready, d, n)
                    relu_lo(h2_ready, h2_lo_ready, d, n)
                c_x4(c)
                c_sum(d)
                norm_stats(3, d.m.yo, d)
                c_x4(d)

            head()
            body(2, lane_before=A_SPARE)
            with dve.Fori(3, GROUPS) as g:
                body(g)
            tail()

        @block.gpsimd
        def _(pool):
            def split_x(t):
                if not t.first:
                    pool.wait_ge(xw0_mm, t.at(1, 0))
                pool.wait_ge(xt_loaded, t.at(16))
                one = ones[:, 0:1].unsqueeze(1).unsqueeze(1).broadcast_to([P, C, G, P])
                pool.tensor_tensor(t.m.xa_hi[:], t.m.xa_t[:], one, ALU.mult).then_inc(xa_hi_ready, 1)
                pool.wait_ge(xa_hi_ready, t.at(1))
                pool.tensor_tensor(t.m.xa_lo[:], t.m.xa_t[:], t.m.xa_hi[:].bitcast(F32), ALU.subtract)\
                    .then_inc(xa_lo_ready, 1)

            def c_bias(t):
                pool.wait_ge(x_ready[2], t.at(2))
                b3_all = b3_rows[:].unsqueeze(1).broadcast_to([P, G, D])
                pool.tensor_tensor(t.m.x3b[:], t.m.x3[:], b3_all, ALU.add).then_inc(x3b_ready, 1)

            def norm_scale(n, t):
                pool.wait_ge(ve_ready[n], t.at(1))
                pool.tensor_tensor(t.m.rs[n][:], t.m.ve[n][:], neg_half[:], ALU.pow).then_inc(rs_ready[n], 1)

            def head():
                pool.memset(act_seed[:], 0.0).then_inc(seed_ready, 1)
                pool.memset(ident[:], 0.0).then_inc(consts, 1)
                pool.memset(ones[:], 1.0).then_inc(consts, 1)
                pool.memset(neg_half[:], -0.5).then_inc(consts, 1)
                pool.wait_ge(consts, 3)
                pool.affine_select(out=ident[:], in_=ident[:], compare_op=ALU.not_equal, fill=1.0, base=0,
                                   pattern=[[-1, P]], channel_multiplier=1).then_inc(ident_ready, 1)
                pool.tensor_copy(ones_r[:], ones[0:2, :]).then_inc(consts, 2)
                pool.memset(c_t[:], 0.0).then_inc(c_zeroed, 1)
                a0, a1 = Turn(pool, 0, A_LANE), Turn(pool, 1, A_SPARE)
                pool.wait_ge(xa_lo_ready, a0.at(1))
                split_x(a1)
                norm_scale(0, a0)
                norm_scale(0, a1)
                split_x(Turn(pool, 2, A_LANE))
                norm_scale(1, a0)
                norm_scale(1, a1)
                pool.wait_ge(rest_loaded, 16 * len(rest_loads))

            def body(g, more=True):
                a, c = Turn(pool, g, A_LANE), Turn(pool, g - 2, C_LANE)
                norm_scale(2, c)
                norm_scale(0, a)
                c_bias(c)
                if more:
                    split_x(Turn(pool, g + 1, A_LANE))
                norm_scale(3, c)
                norm_scale(1, a)

            def tail():
                c, d = Turn(pool, GROUPS - 2, C_LANE), Turn(pool, GROUPS - 1, C_SPARE)
                norm_scale(2, c)
                c_bias(c)
                norm_scale(2, d)
                c_bias(d)
                norm_scale(3, c)
                norm_scale(3, d)

            head()
            body(2)
            with pool.Fori(3, GROUPS - 1) as g:
                body(g)
            body(GROUPS - 1, more=False)
            tail()


_OUT = (B, P, D)


def kernel(x, adj, L0_gnn_Wv, L0_gnn_bv, L0_gnn_aw, L0_gnn_ab, L0_gnn_Wk, L0_gnn_bk, L1_gnn_Wp, L1_gnn_bp,
           L1_gnn_C, L2_gnn_W_qk, L2_gnn_W_v, L3_gnn_W1, L3_gnn_b1, L3_gnn_W2, L3_gnn_b2, L3_gnn_W3, L3_gnn_b3):
    import numpy as np
    import concourse.bacc as bacc
    from concourse.bass_utils import run_bass_kernel_spmd

    def lay(a, shape, order):
        return np.ascontiguousarray(np.asarray(a).reshape(shape).transpose(order))

    def chunks(w):
        w = np.asarray(w)
        return lay(w, (C, P, w.shape[1]), (1, 0, 2))

    wk, qk = np.asarray(L0_gnn_Wk), np.asarray(L2_gnn_W_qk)
    wp = lay(L1_gnn_Wp, (H, D, DH), (1, 0, 2)).reshape(D, D)
    qkv = np.concatenate([np.asarray(L2_gnn_W_v), qk]).T
    wraw = np.concatenate([chunks(w).reshape(P, -1) 
                           for w in (wk[2], wk[1], wk[0], wp, qkv, L3_gnn_W1, L3_gnn_W2, L3_gnn_W3)], axis=1)
    arrays = {
        "x": np.ascontiguousarray(np.asarray(x)),
        "xT": lay(x, (GROUPS, G, P, C, P), (0, 4, 3, 1, 2)),
        "aT": lay(adj, (GROUPS, G, P, P), (0, 3, 1, 2)),
        "wraw": np.ascontiguousarray(wraw),
        "wvT": chunks(np.asarray(L0_gnn_Wv).T),
        "awc": lay(L0_gnn_aw, (2, C, P), (2, 0, 1)),
        "bvc": lay(L0_gnn_bv, (C, P), (1, 0)),
        "ab": np.ascontiguousarray(np.broadcast_to(np.asarray(L0_gnn_ab).reshape(1, 1), (P, 1))),
        "bk": lay(L0_gnn_bk, (1, 3, D), (0, 1, 2)),
        "bpc": lay(L1_gnn_bp, (C, P), (1, 0)),
        "cT": lay(L1_gnn_C, (H, DH, DH), (0, 2, 1)),
        "b1c": lay(L3_gnn_b1, (C, P), (1, 0)),
        "b2c": lay(L3_gnn_b2, (C, P), (1, 0)),
        "b3": np.ascontiguousarray(np.broadcast_to(np.asarray(L3_gnn_b3).reshape(1, D), (P, D))),
    }
    nc = bacc.Bacc("TRN2", target_bir_lowering=False, num_devices=1)
    args = [nc.dram_tensor(f"in_{n}", a.shape, mybir.dt.from_np(a.dtype), kind="ExternalInput").ap()
            for n, a in arrays.items()]
    args.append(nc.dram_tensor("out", _OUT, F32, kind="ExternalOutput").ap())
    build(nc, *args)
    r = run_bass_kernel_spmd(nc, [{f"in_{n}": a for n, a in arrays.items()}], core_ids=[0])
    return r.results[0]["out"]
```
